# Optimizing a Trainium2 kernel written in Bass

```python
import numpy as np
import jax
import jax.numpy as jnp

def _softmax(x, axis=-1):
    return jax.nn.softmax(x, axis=axis)

def _gelu(x):
    return jax.nn.gelu(x, approximate=True)

def _silu(x):
    return jax.nn.silu(x)

def _sigmoid(x):
    return jax.nn.sigmoid(x)

def _layernorm(x, axis=-1, eps=1e-05):
    m = jnp.mean(x, axis=axis, keepdims=True)
    v = jnp.var(x, axis=axis, keepdims=True)
    return (x - m) / jnp.sqrt(v + eps)

def _scatter_add(tgt, idx, src, axis=0):
    return tgt.at[idx].add(src)

def _segment_sum(src, seg, n):
    return jax.ops.segment_sum(src, seg, n)
kernel_name = 'mk_early_fusion_d1_tok_img512_r4_d4a8a2'

def setup_inputs(seed: int=0):
    np.random.seed(seed)
    _w = jnp.asarray

    def _rec_inputs():
        import jax
        import jax.numpy as jnp
        _rk = jax.random.key(seed)
        x = -8.26831e-05 + 0.999903 * jax.random.normal(jax.random.fold_in(_rk, 1), (4, 128, 112, 112), jnp.float32)
        txt = -0.00141891 + 0.32329 * jax.random.normal(jax.random.fold_in(_rk, 2), (4, 128, 128), jnp.float32)
        return (x, txt)
    x, txt = _rec_inputs()

    def _L0_tok_setup():
        import jax, jax.numpy as jnp
        import numpy as np
        SHIFT = 1
        PATCH = 2
        key = jax.random.key(seed)
        k1, k2, k3, k4, k5 = jax.random.split(key, 5)
        B, C, H, W = (32, 128, 112, 112)
        out_c = 2 * C
        patch_dim = out_c * PATCH * PATCH
        dim = 128
        return {'x': jax.random.normal(k1, (B, C, H, W), dtype=jnp.float32), 'conv_w': jax.random.normal(k2, (out_c, 5 * C), dtype=jnp.float32) * 0.02, 'conv_b': jax.random.normal(k3, (out_c,), dtype=jnp.float32) * 0.02, 'lin_w': jax.random.normal(k4, (dim, patch_dim), dtype=jnp.float32) * 0.02, 'lin_b': jax.random.normal(k5, (dim,), dtype=jnp.float32) * 0.02}
    _L0_tok_all = _L0_tok_setup()
    _L0_tok_in = {k: v for k, v in _L0_tok_all.items() if k in ('conv_w', 'conv_b', 'lin_w', 'lin_b')}
    del _L0_tok_all

    def _L0_attn_setup():
        import jax, jax.numpy as jnp
        import numpy as np
        import math
        D_MODEL = 128
        NUM_HEADS = 8
        D_HEAD = D_MODEL // NUM_HEADS
        key = jax.random.key(seed)
        ks = jax.random.split(key, 8)
        B, S = (2, 512)
        x = jax.random.normal(ks[0], (B, S, D_MODEL), dtype=jnp.float32)
        s = 1.0 / math.sqrt(D_MODEL)
        Wq = jax.random.normal(ks[1], (NUM_HEADS, D_MODEL, D_HEAD), dtype=jnp.float32) * s
        Wk = jax.random.normal(ks[2], (NUM_HEADS, D_MODEL, D_HEAD), dtype=jnp.float32) * s
        Wv = jax.random.normal(ks[3], (NUM_HEADS, D_MODEL, D_HEAD), dtype=jnp.float32) * s
        bq = jax.random.normal(ks[4], (NUM_HEADS, D_HEAD), dtype=jnp.float32) * 0.02
        bk = jax.random.normal(ks[5], (NUM_HEADS, D_HEAD), dtype=jnp.float32) * 0.02
        bv = jax.random.normal(ks[6], (NUM_HEADS, D_HEAD), dtype=jnp.float32) * 0.02
        Wo = jax.random.normal(ks[7], (D_MODEL, D_MODEL), dtype=jnp.float32) * s
        bo = jnp.zeros((D_MODEL,), dtype=jnp.float32)
        return {'x': x, 'Wq': Wq, 'Wk': Wk, 'Wv': Wv, 'bq': bq, 'bk': bk, 'bv': bv, 'Wo': Wo, 'bo': bo}
    _L0_attn_all = _L0_attn_setup()
    _L0_attn_in = {k: v for k, v in _L0_attn_all.items() if k in ('Wq', 'Wk', 'Wv', 'bq', 'bk', 'bv', 'Wo', 'bo')}
    del _L0_attn_all

    def _L0_ffn_setup():
        import jax, jax.numpy as jnp
        import numpy as np
        import math
        D_MODEL = 128
        N_EXPERTS = 128
        TOP_K = 8
        N_HEADS = 8
        D_KEYS = 128
        HALF = D_KEYS // 2
        N_BATCH, T_SEQ = (2, 512)
        key = jax.random.key(seed)
        k1, k2, k3, k4, k5, k6 = jax.random.split(key, 6)
        queries = jax.random.normal(k1, (N_BATCH, T_SEQ, D_MODEL), dtype=jnp.float32)
        bound_q = 1.0 / math.sqrt(D_MODEL)
        Wq = jax.random.uniform(k2, (N_HEADS * D_KEYS, D_MODEL), minval=-bound_q, maxval=bound_q, dtype=jnp.float32)
        bq = jax.random.uniform(k3, (N_HEADS * D_KEYS,), minval=-bound_q, maxval=bound_q, dtype=jnp.float32)
        bound_k = 1.0 / math.sqrt(HALF)
        keys = jax.random.uniform(k4, (N_HEADS, 2, N_EXPERTS, HALF), minval=-bound_k, maxval=bound_k, dtype=jnp.float32)
        std = D_MODEL ** (-0.5)
        w_down_embed = std * jax.random.normal(k5, (N_EXPERTS * N_EXPERTS, D_MODEL), dtype=jnp.float32)
        w_up_embed = std * jax.random.normal(k6, (N_EXPERTS * N_EXPERTS, D_MODEL), dtype=jnp.float32)
        return {'queries': queries, 'Wq': Wq, 'bq': bq, 'keys': keys, 'w_down_embed': w_down_embed, 'w_up_embed': w_up_embed}
    _L0_ffn_all = _L0_ffn_setup()
    _L0_ffn_in = {k: v for k, v in _L0_ffn_all.items() if k in ('Wq', 'bq', 'keys', 'w_down_embed', 'w_up_embed')}
    del _L0_ffn_all
    return {'x': x, 'txt': txt, 'L0_tok_conv_w': _L0_tok_in['conv_w'], 'L0_tok_conv_b': _L0_tok_in['conv_b'], 'L0_tok_lin_w': _L0_tok_in['lin_w'], 'L0_tok_lin_b': _L0_tok_in['lin_b'], 'L0_attn_Wq': _L0_attn_in['Wq'], 'L0_attn_Wk': _L0_attn_in['Wk'], 'L0_attn_Wv': _L0_attn_in['Wv'], 'L0_attn_bq': _L0_attn_in['bq'], 'L0_attn_bk': _L0_attn_in['bk'], 'L0_attn_bv': _L0_attn_in['bv'], 'L0_attn_Wo': _L0_attn_in['Wo'], 'L0_attn_bo': _L0_attn_in['bo'], 'L0_ffn_Wq': _L0_ffn_in['Wq'], 'L0_ffn_bq': _L0_ffn_in['bq'], 'L0_ffn_keys': _L0_ffn_in['keys'], 'L0_ffn_w_down_embed': _L0_ffn_in['w_down_embed'], 'L0_ffn_w_up_embed': _L0_ffn_in['w_up_embed']}

def reference(x, txt, L0_tok_conv_w, L0_tok_conv_b, L0_tok_lin_w, L0_tok_lin_b, L0_attn_Wq, L0_attn_Wk, L0_attn_Wv, L0_attn_bq, L0_attn_bk, L0_attn_bv, L0_attn_Wo, L0_attn_bo, L0_ffn_Wq, L0_ffn_bq, L0_ffn_keys, L0_ffn_w_down_embed, L0_ffn_w_up_embed):
    import jax
    import jax.numpy as jnp

    def _L0_tok_ref(x, conv_w, conv_b, lin_w, lin_b):
        import jax, jax.numpy as jnp
        import numpy as np
        SHIFT = 1
        PATCH = 2
        s = SHIFT
        xp = jnp.pad(x, ((0, 0), (0, 0), (s, s), (s, s)))
        x_l = xp[:, :, s:-s, :-2 * s]
        x_r = xp[:, :, s:-s, 2 * s:]
        x_t = xp[:, :, :-2 * s, s:-s]
        x_b = xp[:, :, 2 * s:, s:-s]
        x_cat = jnp.concatenate([x, x_l, x_r, x_t, x_b], axis=1)
        out = jnp.einsum('bchw,oc->bohw', x_cat, conv_w) + conv_b[None, :, None, None]
        B, C2, H, W = out.shape
        p = PATCH
        out = out.reshape(B, C2, H // p, p, W // p, p)
        out = out.transpose(0, 2, 4, 3, 5, 1).reshape(B, H // p * (W // p), p * p * C2)
        return out @ lin_w.T + lin_b

    def _L0_attn_ref(x, Wq, Wk, Wv, bq, bk, bv, Wo, bo):
        import jax, jax.numpy as jnp
        import numpy as np
        import math
        D_MODEL = 128
        NUM_HEADS = 8
        D_HEAD = D_MODEL // NUM_HEADS
        Q = jnp.einsum('bsd,hde->bhse', x, Wq) + bq[None, :, None, :]
        K = jnp.einsum('bsd,hde->bhse', x, Wk) + bk[None, :, None, :]
        V = jnp.einsum('bsd,hde->bhse', x, Wv) + bv[None, :, None, :]
        scale = 1.0 / math.sqrt(D_HEAD)
        scores = jnp.einsum('bhqe,bhke->bhqk', Q, K) * scale
        attn = jax.nn.softmax(scores, axis=-1)
        out = jnp.einsum('bhqk,bhke->bhqe', attn, V)
        B, H, S, d = out.shape
        concat = out.transpose(0, 2, 1, 3).reshape(B, S, H * d)
        return jnp.einsum('bsd,de->bse', concat, Wo) + bo

    def _L0_ffn_ref(queries, Wq, bq, keys, w_down_embed, w_up_embed):
        import jax, jax.numpy as jnp
        import numpy as np
        import math
        D_MODEL = 128
        N_EXPERTS = 128
        TOP_K = 8
        N_HEADS = 8
        D_KEYS = 128
        HALF = D_KEYS // 2
        N_BATCH, T_SEQ = (2, 512)
        N, T, D = queries.shape
        H, E, K = (N_HEADS, N_EXPERTS, TOP_K)
        q_tok = queries.reshape(-1, D)
        qh = q_tok @ Wq.T + bq
        qh = qh.reshape(-1, H, 2, HALF)
        sub_scores = jnp.einsum('nhcf,hcef->nhce', qh, keys)
        s, idx = jax.lax.top_k(sub_scores, K)
        all_scores = (s[:, :, 0, :, None] + s[:, :, 1, None, :]).reshape(-1, H, K * K)
        all_idx = (idx[:, :, 0, :, None] * E + idx[:, :, 1, None, :]).reshape(-1, H, K * K)
        best_s, best_pos = jax.lax.top_k(all_scores, K)
        indices = jnp.take_along_axis(all_idx, best_pos, axis=-1)
        w_down = w_down_embed[indices]
        w_up = w_up_embed[indices]
        x = jnp.einsum('nd,nhkd->nhk', q_tok, w_down)
        x = jax.nn.gelu(x)
        vals = x * jax.nn.softmax(best_s, axis=-1)
        out = jnp.einsum('nhk,nhkd->nd', vals, w_up)
        return out.reshape(N, T, D)
    h = _L0_tok_ref(x, L0_tok_conv_w, L0_tok_conv_b, L0_tok_lin_w, L0_tok_lin_b)
    h = jnp.concatenate([h, txt], axis=1)
    h = h + _L0_attn_ref(_layernorm(h, axis=-1), L0_attn_Wq, L0_attn_Wk, L0_attn_Wv, L0_attn_bq, L0_attn_bk, L0_attn_bv, L0_attn_Wo, L0_attn_bo)
    h = h + _L0_ffn_ref(_layernorm(h, axis=-1), L0_ffn_Wq, L0_ffn_bq, L0_ffn_keys, L0_ffn_w_down_embed, L0_ffn_w_up_embed)
    return h

_drawn_inputs = setup_inputs


def setup_inputs(seed=0):
    import zlib

    import numpy as np

    out = dict(_drawn_inputs(seed))
    spreads = {'L0_attn_bo': (0.0, 0.1)}
    factors = {'L0_attn_bq': 2.884, 'L0_attn_bk': 8.0}
    for name, (base, spread) in spreads.items():
        noise = np.random.default_rng([zlib.crc32(name.encode()), seed]).standard_normal(out[name].shape)
        drawn = base * np.exp(spread * noise) if base else spread * noise
        out[name] = jnp.asarray(drawn.astype(out[name].dtype))
    for name, factor in factors.items():
        out[name] = (out[name] * factor).astype(out[name].dtype)
    return out
```

```python
from contextlib import ExitStack

import concourse.bass as bass
from concourse import mybir

F32 = mybir.dt.float32
BF16 = mybir.dt.bfloat16
U32 = mybir.dt.uint32
ACT = mybir.ActivationFunctionType
ALU = mybir.AluOpType
AX_X = mybir.AxisListType.X

P = 128
B, C, IMG = 4, 128, 112
D = 128
H, E = 8, 16
NP = IMG // 2
NTXT = 128
NTOK = NP * NP + NTXT
NT = -(-NTOK // P)
NPAD = NT * P
Q = 256
SUP = NPAD // Q
G_ALL = B * SUP
FH, TOPK, NE = 8, 8, 128
EPS = 1e-5

KPART = (0, 0, 1, 1, 0, 2)
QPART = (0, 1, 0, 1, 2, 0)
SROWS = len(KPART) * E
SHIFT = SROWS

SHIFTS = ((0, 0), (0, -1), (0, 1), (-1, 0), (1, 0))
TAPS = {}
for _py in range(2):
    for _px in range(2):
        for _s, (_dy, _dx) in enumerate(SHIFTS):
            TAPS.setdefault((_py + _dy, _px + _dx), []).append((_py * 2 + _px, _s))
TAP_ORDER = sorted(TAPS, key=lambda t: (t[0] not in (0, 1)) or (t[1] not in (0, 1)))

PROWS = 8
NTOKSTEP = NP // PROWS
TSTEP = PROWS * NP
CH = 512
NCH = -(-NTOK // CH)
CW = [min(CH, NTOK - c * CH) for c in range(NCH)]
CT = [-(-w // P) for w in CW]
QUADS = [(q * 4, min(4, NT - q * 4)) for q in range(-(-NT // 4))]
NQ = len(QUADS)
XCH = NT // 2

PER_R = H * 2 * NCH + 2 * 4
PER_X = H * XCH
PER_MA, PER_MD = 14, 10
PAIR = 16
NPAIR = 2 * FH * TOPK // PAIR
PER_UP = NPAIR * PAIR
RING = 4
R_SPLIT = (3, 3, 3, 3, 2, 0, 0)
DOT_SPLIT = (0, 0, 2, 2, 3, 4, 5)
UP_SPLIT = (0, 2, 3, 3, 3, 3, 2)
GELU_C = 2.0 * 0.7978845608028654
RSQRT_SEED = float(0x5F3759DF)
PAIR_DVE = PAIR + 5
EXP_DVE = 3 + NPAIR * PAIR_DVE
SETUP_DVE = 18
BUILD_DVE = 140
ATT_DVE = 97


def first(b):
    return isinstance(b, int) and b == 0


def misc_m(h):
    return 6 if h == 0 else 5 + 2 * h


def misc_o(h):
    return 8 + 2 * h if h < H - 1 else 21


def dma_count(b, n, per=(NTOKSTEP + 1) // 2, other=NTOKSTEP // 2):
    return 16 * (b * (per if n % 2 == 0 else other) + n // 2 + 1)


class Tally:

    def __init__(self, per):
        self.per, self.base, self.k = per, 0, 0

    def begin(self, index):
        self.base, self.k = index * self.per, 0

    def __call__(self, instruction):
        self.k += 1
        return self.base + self.k

    def end(self):
        assert self.k == self.per, (self.k, self.per)


def early_fusion(nc, x, txt, conv_w, conv_b, lin_wt, lin_b, wq, wk, wv, bq, bk, bvo, wo,
                 ffn_wq, ffn_bq, ffn_keys_t, table, ident, sel_w, sel_v, part_masks, iota8, out):
    with ExitStack() as ctx:
        def sb(name, shape, dt):
            return ctx.enter_context(nc.sbuf_tensor(name, shape, dt))

        def sem(name):
            return ctx.enter_context(nc.semaphore(name))

        kst = sb("key_stack", [P, H, NPAD], BF16)
        vals_sb = sb("values", [P, NT * H * 17 + 15], F32)
        v4 = vals_sb[:, 0:NT * H * 17].rearrange("p (t h c) -> p t h c", t=NT, c=17)
        h_t = sb("h_t", [P, NPAD], F32)
        gat = sb("gathered", [P, RING * PAIR, 2 * D], F32)
        qst = sb("query_stack", [P, H, Q], BF16)
        xrow = (qst[:, :, :].rearrange("p h q -> p (h q)").bitcast(F32)
                .rearrange("p (c t d) -> p c t d", c=2, t=4))
        probs = sb("probs", [P, 4, 2 * Q], F32)
        diag = sb("diag", [P, 8, D], F32)
        hrow = diag[:, :, :].rearrange("p (c t) d -> p c t d", c=2)
        slab = [sb(f"slab{i}", [P, 2 * PROWS + 2, IMG], F32) for i in range(1)]
        slab.append(probs[:, :, :].rearrange("p a b -> p (a b)")[:, 0:(2 * PROWS + 2) * IMG]
                    .rearrange("p (r w) -> p r w", w=IMG))
        w_tap = sb("w_tap", [P, 12, D], F32)
        w_s = sb("w_s", [P, FH * 2 * NE], F32)
        wq_sb = sb("wq_sb", [P, D], F32)
        wk_sb = sb("wk_sb", [P, D], F32)
        wv_sb = sb("wv_sb", [P, D], F32)
        wo_sb = sb("wo_sb", [P, D], F32)
        cols = sb("cols", [P, 4], F32)
        brow = sb("brow", [3, FH * 2 * NE + 2 * D], BF16)
        idf = sb("idf", [P, P], F32)
        idb = sb("idb", [P, P], BF16)
        selw = sb("selw", [P, H, 4 * E], BF16)
        selv = sb("selv", [P, 17], F32)
        masks = sb("masks", [3, 2], F32)
        iot = sb("iot", [P, 8], F32)
        ones3 = sb("ones3", [3, P], BF16)
        shared = sb("shared", [P, 3 * CH // 2], F32)
        parts = shared[:, :].bitcast(BF16).rearrange("p (a n) -> p a n", a=3)
        o_n = shared[:, 0:2 * D].rearrange("p (a d) -> p a d", a=2)
        c_t = shared[:, 2 * D:2 * D + Q]
        s8 = shared[:, 512:640].rearrange("p (h c k) -> p h c k", h=FH, c=2)
        i8 = shared[:, 640:768].bitcast(U32).rearrange("p (h c k) -> p h c k", h=FH, c=2)
        st = sb("st", [P, 4, 6], F32)
        mv = sb("mv", [P, 4, 2], F32)
        ln = sb("ln", [P, 6, 4], F32)
        lnu = sb("lnu", [P, 2, 4], U32)
        hres = sb("hres", [P, 2, D], F32)
        mxp = sb("mxp", [P, 2, NCH], F32)
        mx = sb("mx", [P, 2, 2], F32)
        mneg = sb("mneg", [P, 2, 32], BF16)
        o_t = sb("o_t", [P, Q], F32)
        rcp = sb("rcp", [P, 2, 1], F32)
        h1n = sb("h1n", [P, 2, D], F32)
        h1c = sb("h1c", [P, 2, D], F32)
        x2n = sb("x2n", [P, 2, D], F32)
        x2c = sb("x2c", [P, 2, D], F32)
        x2t = c_t
        i8f = sb("i8f", [P, FH, 2, 8], F32)
        b8 = sb("b8", [P, FH, 8], F32)
        p8 = sb("p8", [P, FH, 8], U32)
        pij = sb("pij", [P, 2, FH * 8], U32)
        oneh = sb("oneh", [P, FH, 8, 8], F32)
        work_f = oneh[:, :, :, :].rearrange("p h k i -> p (h k i)")
        picked = sb("picked", [P, 2, FH * 8], F32)
        wsm = sb("wsm", [P, 2, FH, 8], F32)
        wsum = sb("wsum", [P, FH], F32)
        wn = sb("wn", [P, 2, FH * 8], F32)
        wc = sb("wc", [P, 2, FH * 8], F32)
        idx = [sb(f"idx{a}", [P, FH * 8], U32) for a in range(2)]
        xd = sb("xd", [P, PAIR], F32)
        gz = sb("gz", [P, 4, PAIR], F32)
        ge = sb("ge", [P, PAIR], F32)
        gv = sb("gv", [P, PAIR], F32)
        ostage = sb("ostage", [P, 2, D], F32)
        txt_sb = o_t[:, 0:D]

        gflat = gat[:, :, :].rearrange("p a b -> p (a b)")
        cw = gflat[:, 0:1280].rearrange("p (o n) -> p o n", o=2)
        lw = gflat[:, 1280:2304].rearrange("p (k d) -> p k d", k=8)
        fq = gflat[:, 2304:3328].rearrange("p (h d) -> p h d", h=FH)
        fk = gflat[:, 3328:4352].rearrange("p (h e) -> p h e", h=FH)
        fb = gflat[:, 4352:4376].rearrange("p (h r) -> p h r", h=FH)
        cb = gflat[:, 4376:4378]
        NB = FH * 2 * NE + 2 * D
        brf = gflat[0:3, 4400:4400 + NB]
        brt = gflat[0:3, 6800:6800 + NB]
        selw_f = gflat[:, 9200:9200 + H * 4 * E]
        brh = gflat[0:3, 14000:14000 + NB // 2].bitcast(BF16)

        bank = [ctx.enter_context(nc.psum_tensor(f"bank{i}", [P, 512], F32)) for i in range(8)]
        RB, XB, PV, UP, MISC = bank[0:2], bank[2:5], bank[5], bank[6], bank[7]

        h_dram = nc.dram_tensor("h_rows", [B * NPAD, D], F32, kind="Internal").ap()

        const_in = sem("const_in")
        table_in = sem("table_in")
        set_pe = sem("set_pe")
        set_act = sem("set_act")
        set_dve = sem("set_dve")
        slab_in = [sem("slab_in0"), sem("slab_in1")]
        txt_in = sem("txt_in")
        txt_ready = sem("txt_ready")
        tok_ready = sem("tok_ready")
        tok_copied = sem("tok_copied")
        lnt_ready = sem("lnt_ready")
        hrow_ready = sem("hrow_ready")
        hrow_stored = [sem("hrow_stored0"), sem("hrow_stored1")]
        xrow_ready = sem("xrow_ready")
        xt_ready = sem("xt_ready")
        xt_copied = sem("xt_copied")
        k_ready = sem("k_ready")
        kf_ready = sem("kf_ready")
        kparts_ready = sem("kparts_ready")
        v_ready = sem("v_ready")
        v_copied = sem("v_copied")
        place_ready = sem("place_ready")
        place_dve = sem("place_dve")
        place_act = sem("place_act")
        build_dve = sem("build_dve")
        hres_in = sem("hres_in")
        misc_ready = sem("misc_ready")
        misc_act = sem("misc_act")
        misc_dve = sem("misc_dve")
        qparts_ready = sem("qparts_ready")
        r_ready = sem("r_ready")
        r_free = sem("r_free")
        mneg_ready = sem("mneg_ready")
        x_ready = sem("x_ready")
        exp_done = sem("exp_done")
        pv_done = sem("pv_done")
        ot_ready = sem("ot_ready")
        o_ready = sem("o_ready")
        x2_ready = sem("x2_ready")
        h1_ready = sem("h1_ready")
        best_ready = sem("best_ready")
        bexp_ready = sem("bexp_ready")
        att_dve = sem("att_dve")
        idx_ready = sem("idx_ready")
        rows_in = [sem(f"rows_in{i}") for i in range(2 * RING)]
        z_ready = sem("z_ready")
        e_ready = sem("e_ready")
        val_ready = sem("val_ready")
        diag_ready = sem("diag_ready")
        up_done = sem("up_done")
        out_ready = sem("out_ready")
        out_stored = [sem("out_stored0"), sem("out_stored1")]
        exp_dve = sem("exp_dve")

        N_CONST = 19

        def schedule(eng, setup, build, supertile):
            setup()
            build(0)
            supertile(0, 0, True, False, False)
            supertile(1, 1, True, True, False)
            with eng.Fori(2, SUP) as s:
                supertile(s, s, True, True, True)
            with eng.Fori(1, B) as b:
                build(b)
                supertile(b * SUP, 0, True, True, True)
                with eng.Fori(1, SUP) as s:
                    supertile(b * SUP + s, s, True, True, True)
            supertile(G_ALL, None, False, True, True)
            supertile(G_ALL + 1, None, False, False, True)

        passed = {nc.vector: sem("passed_dve"), nc.gpsimd: sem("passed_pool"), nc.sync: sem("passed_sp")}

        def settled(eng):
            eng.sem_inc(passed[eng], 1)

        block = ctx.enter_context(nc.Block())

        @block.sync
        def _(sp):
            def setup():
                pairs = [
                    (cw, conv_w.rearrange("(o p) n -> p o n", p=P)),
                    (lw, lin_wt.rearrange("(k p) d -> p k d", p=P)),
                    (cb, conv_b),
                    (fq, ffn_wq.rearrange("(h p) d -> p h d", p=P)),
                    (fk, ffn_keys_t.rearrange("c f h e -> (c f) h e")),
                    (fb, ffn_bq.rearrange("(h p) r -> p h r", p=P)),
                    (wq_sb[:, :], wq), (wk_sb[:, :], wk), (wv_sb[:, :], wv), (wo_sb[:, :], wo),
                    (cols[:, 0:1], bq), (cols[:, 1:2], bk), (cols[:, 3:4], lin_b),
                    (brf[:, FH * 2 * NE:], bvo),
                    (idf[:, :], ident),
                    (selw_f, sel_w), (selv[:, :], sel_v),
                    (masks[:, :], part_masks), (iot[:, :], iota8),
                ]
                assert len(pairs) == N_CONST, len(pairs)
                for dst, src in pairs:
                    sp.dma_start(dst, src).then_inc(const_in, 16)

            def build(b):
                def load_slab(n):
                    i = n % 2
                    if n >= 2:
                        sp.wait_ge(tok_ready, b * NTOKSTEP + n - 1)
                    elif not first(b):
                        sp.wait_ge(tok_ready, b * NTOKSTEP)
                        sp.wait_ge(pv_done, b * SUP * PER_X)
                    lo, hi = max(0, 2 * PROWS * n - 1), min(IMG, 2 * PROWS * (n + 1) + 1)
                    at = 1 if n == 0 else 0
                    sp.dma_start(slab[i][:, at:at + hi - lo, :],
                                 x[bass.ds(b, 1), :, lo:hi, :].rearrange("b c r w -> (b c) r w")).then_inc(slab_in[i], 16)

                load_slab(0)
                load_slab(1)
                if not first(b):
                    sp.wait_ge(misc_ready, b * SUP * 24)
                sp.dma_start(txt_sb, txt[bass.ds(b, 1), :, :].rearrange("b t d -> (b t) d")).then_inc(txt_in, 16)
                for c in range(NCH):
                    if c + 2 < NTOKSTEP:
                        load_slab(c + 2)
                    sp.wait_ge(hrow_ready, b * NCH + c + 1)
                    rows = h_dram[bass.ds(b * NPAD + c * CH, CT[c] * P), :]
                    sp.dma_start(rows.rearrange("(t p) d -> p t d", p=P), hrow[:, c % 2, 0:CT[c], :])\
                        .then_inc(hrow_stored[c % 2], 16)
                sp.wait_ge(hrow_stored[0], dma_count(b, NCH - 1))
                sp.wait_ge(hrow_stored[1], dma_count(b, NCH - 2))
                settled(sp)

            def supertile(g, s, att, ffn, fin):
                if att:
                    if not (isinstance(g, int) and g == 0):
                        sp.wait_ge(h1_ready, g)
                    sp.dma_start(hres[:, :, :], h_dram[bass.ds(g * Q, Q), :].rearrange("(t p) d -> p t d", p=P))\
                        .then_inc(hres_in, 16)
                if fin:
                    sp.wait_ge(out_ready, (g - 2) * 2 + 2)
                    sp.dma_start(out[bass.ds((g - 2) * Q + P, P), :], ostage[:, 1, :]).then_inc(out_stored[1], 16)
                if ffn:
                    sp.wait_ge(out_ready, (g - 1) * 2 + 1)
                    sp.dma_start(out[bass.ds((g - 1) * Q, P), :], ostage[:, 0, :]).then_inc(out_stored[0], 16)

            schedule(sp, setup, build, supertile)
            for o in out_stored:
                sp.wait_ge(o, 16 * G_ALL)

        @block.gpsimd
        def _(pool):
            def gather(f, first_f):
                for j in range(NPAIR):
                    a = j // 4
                    if j % 4 == 0:
                        pool.wait_ge(idx_ready, f * 2 + a + 1)
                    if not (first_f and j < RING):
                        pool.wait_ge(up_done, f * PER_UP + (j - RING + 1) * PAIR)
                    settled(pool)
                    for k in range(PAIR):
                        col = (j % 4) * PAIR + k
                        pool.indirect_dma_start(
                            gat[:, (j % RING) * PAIR + k, :], None, table,
                            bass.IndirectOffsetOnAxis(ap=idx[a][:, col:col + 1], axis=0),
                        ).then_inc(rows_in[2 * (j % RING) + k // 8], 16)

            gather(0, True)
            with pool.Fori(1, G_ALL) as f:
                gather(f, False)

        @block.scalar
        def _(act):
            def setup():
                act.wait_ge(set_pe, 1)
                for i in range(3):
                    act.activation(w_tap[:, 4 * i:4 * i + 4, :], XB[i][:, :].rearrange("p (t d) -> p t d", d=D),
                                   ACT.Copy).then_inc(set_act, 1)
                act.wait_ge(set_pe, 2)
                ws4 = w_s[:, :].rearrange("p (h c e) -> p h c e", h=FH, c=2)
                for i, bk_ in enumerate((bank[0], bank[1], UP, MISC)):
                    c, hh = i // 2, i % 2
                    act.activation(ws4[:, 4 * hh:4 * hh + 4, c, :], bk_[:, :].rearrange("p (h e) -> p h e", e=NE),
                                   ACT.Copy).then_inc(set_act, 1)
                act.wait_ge(set_pe, 3)
                bs4 = brf[:, 0:FH * 2 * NE].rearrange("p (h c e) -> p h c e", h=FH, c=2)
                for i, bk_ in enumerate((bank[0], bank[1], UP, MISC)):
                    c, hh = i // 2, i % 2
                    act.activation(bs4[:, 4 * hh:4 * hh + 4, c, :], bk_[0:3, :].rearrange("p (h e) -> p h e", e=NE),
                                   ACT.Copy).then_inc(set_act, 1)

            def build(b):
                def tok(n):
                    act.wait_ge(tok_ready, b * NTOKSTEP + n + 1)
                    act.activation(h_t[:, n * TSTEP:(n + 1) * TSTEP], XB[n % 2][:, 0:TSTEP], ACT.Identity,
                                   bias=cols[:, 2:3]).then_inc(tok_copied, 1)

                if first(b):
                    act.wait_ge(set_dve, SETUP_DVE)
                tok(0)
                tok(1)
                for c in range(NCH):
                    w, nt = CW[c], CT[c]
                    if c == NCH - 1:
                        act.wait_ge(txt_ready, b + 1)
                        act.activation(h_t[:, NP * NP:NTOK], XB[2][:, 0:P], ACT.Copy).then_inc(tok_copied, 1)
                    act.wait_ge(lnt_ready, b * NCH + c + 1)
                    if c >= 2:
                        act.wait_ge(hrow_stored[c % 2], dma_count(b, c - 2))
                        act.wait_ge(xrow_ready, b * NCH + c - 1)
                    elif not first(b):
                        act.wait_ge(hrow_stored[c % 2], dma_count(b, c) - 16)
                    act.activation(hrow[:, c % 2, 0:nt, :], RB[c % 2][:, 0:nt * P].rearrange("p (t d) -> p t d", d=D),
                                   ACT.Copy).then_inc(hrow_ready, 1)
                    if c + 2 < NTOKSTEP:
                        tok(c + 2)
                    act.wait_ge(xt_ready, b * NCH + c + 1)
                    act.activation(h_t[:, c * CH:c * CH + nt * P], XB[2][:, 0:nt * P], ACT.Copy).then_inc(xt_copied, 1)
                    act.wait_ge(k_ready, b * NCH + c + 1)
                    if c or not first(b):
                        act.wait_ge(kparts_ready, b * NCH + c)
                    act.activation(work_f[:, 0:w], MISC[:, 0:w], ACT.Identity, bias=cols[:, 1:2]).then_inc(kf_ready, 1)
                    act.wait_ge(v_ready, b * NCH + c + 1)
                    full = w // P
                    last = act.activation(v4[:, 4 * c:4 * c + full, :, 0:E],
                                          PV[:, 0:full * P].rearrange("p (t h e) -> p t h e", t=full, e=E), ACT.Copy)
                    if w % P:
                        r = w % P
                        last.then_inc(v_copied, 1)
                        last = act.activation(v4[0:r, 4 * c + full, :, 0:E],
                                              PV[0:r, full * P:(full + 1) * P].rearrange("p (h e) -> p h e", e=E), ACT.Copy)
                    last.then_inc(v_copied, 1)
                    for h in range(1, H, 2):
                        act.wait_ge(place_ready, (b * NCH + c) * H + h + 1)
                        act.activation(kst[0:SROWS, h, c * CH:c * CH + w], PV[0:SROWS, 0:w], ACT.Copy)\
                            .then_inc(place_act, 1)
                act.wait_ge(hrow_stored[0], dma_count(b, NCH - 1))
                act.wait_ge(hrow_stored[1], dma_count(b, NCH - 2))

            def supertile(g, s, att, ffn, fin):
                md = 0

                def diags(j, f, i0, n):
                    for k in range(i0, i0 + n):
                        u = j * PAIR + k
                        if not (isinstance(f, int) and f == 0 and u < 8):
                            act.wait_ge(up_done, f * PER_UP + u - 7)
                        act.activation(diag[:, u % 8, :], idf[:, :], ACT.Copy, scale=gv[:, k:k + 1]).then_inc(diag_ready, 1)

                def gexp(j, f):
                    act.wait_ge(z_ready, f * NPAIR + j + 1)
                    act.activation(ge[:, :], gz[:, 2, :], ACT.Exp, scale=-GELU_C).then_inc(e_ready, 1)

                def vals(j, f):
                    act.wait_ge(val_ready, f * NPAIR + j + 1)

                def misc_copy(dst, src, k, func=ACT.Copy):
                    act.activation(dst, src, func).then_inc(misc_act, 1)

                if att:
                    for u in range(4):
                        act.wait_ge(misc_ready, g * 24 + 2 + u)
                        act.activation(qst[0:SROWS, 2 * u:2 * u + 2, :],
                                       MISC[0:SROWS, :].rearrange("p (h q) -> p h q", q=Q), ACT.Copy).then_inc(misc_act, 1)
                if fin:
                    gexp(7, g - 2)
                    vals(7, g - 2)
                    diags(7, g - 2, 0, PAIR)

                def mcopy(h, use):
                    act.wait_ge(misc_ready, g * 24 + use)
                    act.activation(qst[SHIFT:P, h, :], MISC[SHIFT:P, 0:Q], ACT.Copy).then_inc(misc_act, 1)

                if att:
                    mcopy(0, 6)
                for h in range(H):
                    j = h - 3
                    if ffn and j >= 0:
                        gexp(j, g - 1)
                    done = 0
                    for q, (t0, nt) in enumerate(QUADS):
                        if att:
                            for i in range(nt // 2):
                                n = h * XCH + t0 // 2 + i
                                act.wait_ge(x_ready, g * PER_X + n + 1)
                                if not (isinstance(g, int) and g == 0 and n < 4):
                                    act.wait_ge(pv_done, g * PER_X + n - 3)
                                act.activation(probs[:, n % 4, :], XB[n % 3][:, :], ACT.Exp, scale=E ** -0.5)\
                                    .then_inc(exp_done, 1)
                        if ffn and j >= 0:
                            if q == 1:
                                vals(j, g - 1)
                            diags(j, g - 1, done, UP_SPLIT[q])
                            done += UP_SPLIT[q]
                    if att:
                        if h < H - 1:
                            mcopy(h + 1, misc_m(h + 1))
                        act.wait_ge(pv_done, g * PER_X + (h + 1) * XCH)
                        if h:
                            act.wait_ge(misc_ready, g * 24 + misc_o(h - 1))
                        act.activation(o_t[:, :], PV[:, 0:Q], ACT.Copy).then_inc(ot_ready, 1)
                if att:
                    act.wait_ge(misc_ready, g * 24 + 22)
                    act.activation(c_t, MISC[:, 0:Q], ACT.Copy).then_inc(misc_act, 1)
                    act.wait_ge(misc_ready, g * 24 + 24)
                    act.activation(x2t, MISC[:, 0:Q], ACT.Copy).then_inc(misc_act, 1)
                for a in range(2):
                    if ffn:
                        gexp(5 + a, g - 1)
                        vals(5 + a, g - 1)
                        diags(5 + a, g - 1, 0, PAIR)
                    if att:
                        act.wait_ge(best_ready, g * 2 + a + 1)
                        act.activation(wsm[:, 1, :, :], wsm[:, 0, :, :], ACT.Exp).then_inc(bexp_ready, 1)

            schedule(act, setup, build, supertile)

        @block.vector
        def _(dve):
            ts = Tally(SETUP_DVE)
            tb = Tally(BUILD_DVE)
            ta = Tally(ATT_DVE)

            def setup():
                def step(ins):
                    dve.wait_ge(set_dve, ts(ins.then_inc(set_dve, 1)))

                step(dve.memset(kst[:, :, NTOK:NPAD], 0.0))
                step(dve.memset(kst[SHIFT:P, :, 0:NTOK], 0.0))
                step(dve.memset(kst[SHIFT:SHIFT + 3, :, 0:NTOK], 1.0))
                step(dve.memset(vals_sb[:, :], 0.0))
                step(dve.memset(v4[:, 0:NT - 1, :, E:E + 1], 1.0))
                step(dve.memset(v4[0:NTOK - (NT - 1) * P, NT - 1, :, E:E + 1], 1.0))
                step(dve.memset(h_t[:, NTOK:NPAD], 0.0))
                step(dve.memset(mneg[:, :, :], 0.0))
                step(dve.memset(ones3[:, :], 1.0))
                dve.wait_ge(const_in, 16 * N_CONST)
                step(dve.tensor_copy(idb[:, :], idf[:, :]))
                step(dve.tensor_copy(selw[:, :, :].rearrange("p h r -> p (h r)"), selw_f))
                dve.wait_ge(set_pe, 1)
                step(dve.tensor_tensor(cols[:, 2:3], PV[:, 0:1], cols[:, 3:4], ALU.add))
                dve.wait_ge(set_act, 11)
                step(dve.tensor_copy(brh, brf))
                step(dve.tensor_scalar(brt, brh, masks[:, 0:1], -1.0, ALU.mult, ALU.mult))
                step(dve.tensor_tensor(brt, brt, brf, ALU.add))
                step(dve.tensor_copy(brh, brt))
                step(dve.tensor_scalar(brf, brh, masks[:, 1:2], -1.0, ALU.mult, ALU.mult))
                step(dve.tensor_tensor(brow[:, :], brf, brt, ALU.add))
                ts.end()

            def split(src, w, tally_step):
                tally_step(dve.tensor_copy(parts[:, 0, 0:w], src))
                tally_step(dve.tensor_tensor(src, src, parts[:, 0, 0:w], ALU.subtract))
                tally_step(dve.tensor_copy(parts[:, 1, 0:w], src))
                return dve.tensor_tensor(parts[:, 2, 0:w], src, parts[:, 1, 0:w], ALU.subtract)

            def rsqrt(n, step):
                v, r, t = ln[:, 0, 0:n], ln[:, 3, 0:n], ln[:, 4, 0:n]
                step(dve.tensor_scalar(v, mv[:, 0:n, 1], EPS, None, ALU.add))
                step(dve.tensor_scalar(lnu[:, 0, 0:n], v.bitcast(U32), 1, None, ALU.logical_shift_right))
                step(dve.tensor_scalar(r.bitcast(U32), lnu[:, 0, 0:n], -1.0, RSQRT_SEED, ALU.mult, ALU.add))
                for _ in range(3):
                    step(dve.tensor_tensor(t, v, r, ALU.mult))
                    step(dve.tensor_tensor(t, t, r, ALU.mult))
                    step(dve.tensor_scalar(t, t, -0.5, 1.5, ALU.mult, ALU.add))
                    step(dve.tensor_tensor(r, r, t, ALU.mult))

            def build(b):
                tb.begin(b)

                def step(ins):
                    dve.wait_ge(build_dve, tb(ins.then_inc(build_dve, 1)))

                for c in range(NCH):
                    w, nt = CW[c], CT[c]
                    dve.wait_ge(hrow_ready, b * NCH + c + 1)
                    for t in range(nt):
                        last = dve.bn_stats(st[:, t, :], hrow[:, c % 2, t, :])
                    dve.wait_ge(build_dve, tb(last.then_inc(build_dve, 1)))
                    settled(dve)
                    for t in range(nt):
                        last = dve.bn_aggr(mv[:, t, :], st[:, t, :])
                    dve.wait_ge(build_dve, tb(last.then_inc(build_dve, 1)))
                    rsqrt(nt, step)
                    if c >= 2 or not first(b):
                        dve.wait_ge(xt_ready, b * NCH + c - 1 if c >= 2 else b * NCH)
                    for t in range(nt):
                        last = dve.tensor_scalar(xrow[:, c % 2, t, :], hrow[:, c % 2, t, :], mv[:, t, 0:1],
                                                 ln[:, 3, t:t + 1], ALU.subtract, ALU.mult)
                    last.then_inc(xrow_ready, 1)
                    dve.wait_ge(xrow_ready, b * NCH + c + 1)
                    dve.wait_ge(kf_ready, b * NCH + c + 1)
                    if c or not first(b):
                        dve.wait_ge(place_ready, (b * NCH + c) * H)
                    split(work_f[:, 0:w], w, step).then_inc(kparts_ready, 1)
                    for h in range(0, H, 2):
                        dve.wait_ge(place_ready, (b * NCH + c) * H + h + 1)
                        dve.tensor_copy(kst[0:SROWS, h, c * CH:c * CH + w], MISC[0:SROWS, 0:w]).then_inc(place_dve, 1)
                tb.end()

            def supertile(g, s, att, ffn, fin):
                ta.begin(g)
                fbase = [0]

                def step(ins):
                    dve.wait_ge(att_dve, ta(ins.then_inc(att_dve, 1)))

                def estep(f, k, ins):
                    ins.then_inc(exp_dve, 1)
                    dve.wait_ge(exp_dve, f * EXP_DVE + k)

                def dots(j, f, k0, n):
                    a = j // 4
                    for k in range(k0, k0 + n):
                        if k % 8 == 0:
                            dve.wait_ge(rows_in[2 * (j % RING) + k // 8], f * 256 + (j // RING + 1) * 128)
                        row = gat[:, (j % RING) * PAIR + k, 0:D]
                        dve.tensor_tensor_reduce(row, x2c[:, a, :], row, 1.0, 0.0, ALU.mult, ALU.add,
                                                 xd[:, k:k + 1]).then_inc(exp_dve, 1)

                def gelu_arg(j, f):
                    k = 3 + j * PAIR_DVE + PAIR
                    dve.wait_ge(exp_dve, f * EXP_DVE + k)
                    if j or not (isinstance(f, int) and f == 0):
                        dve.wait_ge(val_ready, f * NPAIR + j)
                    a, c0 = j // 4, (j % 4) * PAIR
                    estep(f, k + 1, dve.tensor_tensor(gz[:, 0, :], xd[:, :], xd[:, :], ALU.mult))
                    estep(f, k + 2, dve.tensor_scalar(gz[:, 1, :], gz[:, 0, :], 0.044715, 1.0, ALU.mult, ALU.add))
                    dve.tensor_tensor(gz[:, 2, :], gz[:, 1, :], xd[:, :], ALU.mult).then_inc(z_ready, 1)
                    dve.wait_ge(z_ready, f * NPAIR + j + 1)
                    estep(f, k + 3, dve.tensor_tensor(gz[:, 3, :], xd[:, :], wc[:, a, c0:c0 + PAIR], ALU.mult))

                def gelu_val(j, f):
                    k = 3 + j * PAIR_DVE + PAIR + 3
                    dve.wait_ge(e_ready, f * NPAIR + j + 1)
                    estep(f, k + 1, dve.tensor_scalar(gz[:, 0, :], ge[:, :], 1.0, None, ALU.add))
                    estep(f, k + 2, dve.reciprocal(gz[:, 1, :], gz[:, 0, :]))
                    if j or not (isinstance(f, int) and f == 0):
                        dve.wait_ge(diag_ready, f * PER_UP + j * PAIR)
                    dve.tensor_tensor(gv[:, :], gz[:, 1, :], gz[:, 3, :], ALU.mult).then_inc(val_ready, 1)

                def out_add(a, f):
                    dve.wait_ge(up_done, f * PER_UP + (a + 1) * 64)
                    if not (isinstance(f, int) and f == 0):
                        dve.wait_ge(out_stored[a], f * 16)
                    dve.tensor_tensor(ostage[:, a, :], UP[:, 0:D], h1c[:, a, :], ALU.add).then_inc(out_ready, 1)

                rk = [0]

                def reduce(n, h):
                    a, c = n // NCH, n % NCH
                    k = h * 2 * NCH + n
                    dve.wait_ge(r_ready, g * PER_R + k + 1)
                    dve.tensor_reduce(mxp[:, a, c:c + 1], RB[k % 2][:, 0:CW[c]], AX_X, ALU.max).then_inc(r_free, 1)

                def minus_max(h):
                    dve.wait_ge(r_free, g * PER_R + (h + 1) * 2 * NCH)
                    step(dve.tensor_reduce(mx[:, 0, :], mxp[:, :, :], AX_X, ALU.max))
                    if h:
                        dve.wait_ge(misc_ready, g * 24 + misc_m(h - 1))
                    step(dve.tensor_scalar(mneg[:, :, 0], mx[:, 0, :], -1.0, None, ALU.mult))
                    step(dve.scalar_tensor_tensor(out=mx[:, 1, :], in0=mx[:, 0, :], scalar=-1.0, in1=mneg[:, :, 0],
                                                  op0=ALU.mult, op1=ALU.subtract))
                    step(dve.tensor_copy(mneg[:, :, 1], mx[:, 1, :]))
                    dve.tensor_tensor(mneg[:, :, 2], mx[:, 1, :], mneg[:, :, 1], ALU.subtract).then_inc(mneg_ready, 1)

                def norm_head(h):
                    dve.wait_ge(misc_ready, g * 24 + misc_o(h))
                    o3 = MISC[:, 0:34].rearrange("p (a c) -> p a c", a=2)
                    step(dve.reciprocal(rcp[:, :, :], o3[:, :, E:E + 1]))
                    dve.tensor_tensor(o_n[:, :, h * E:(h + 1) * E], o3[:, :, 0:E], rcp[:, :, :].to_broadcast([P, 2, E]),
                                      ALU.mult).then_inc(misc_dve, 1)

                def select(a):
                    for c4 in range(4):
                        k = H * 2 * NCH + 4 * a + c4
                        dve.wait_ge(r_ready, g * PER_R + k + 1)
                        settled(dve)
                        for i in range(4):
                            h, c = 2 * c4 + i // 2, i % 2
                            last = dve.max(s8[:, h, c, :], RB[k % 2][:, i * NE:(i + 1) * NE])
                        dve.wait_ge(att_dve, ta(last.then_inc(att_dve, 1)))
                        settled(dve)
                        for i in range(4):
                            h, c = 2 * c4 + i // 2, i % 2
                            last = dve.max_index(i8[:, h, c, :], s8[:, h, c, :], RB[k % 2][:, i * NE:(i + 1) * NE])
                        last.then_inc(r_free, 1)
                    dve.wait_ge(r_free, g * PER_R + H * 2 * NCH + 4 * a + 4)
                    step(dve.tensor_copy(i8f[:, :, :, :], i8[:, :, :, :]))
                    step(dve.tensor_tensor(oneh[:, :, :, :], s8[:, :, 0, :].unsqueeze(3).to_broadcast([P, FH, 8, 8]),
                                           s8[:, :, 1, :].unsqueeze(2).to_broadcast([P, FH, 8, 8]), ALU.add))
                    settled(dve)
                    for h in range(FH):
                        last = dve.max(b8[:, h, :], oneh[:, h, :, :].rearrange("p i j -> p (i j)"))
                    dve.wait_ge(att_dve, ta(last.then_inc(att_dve, 1)))
                    settled(dve)
                    for h in range(FH):
                        last = dve.max_index(p8[:, h, :], b8[:, h, :], oneh[:, h, :, :].rearrange("p i j -> p (i j)"))
                    dve.wait_ge(att_dve, ta(last.then_inc(att_dve, 1)))
                    dve.tensor_tensor(wsm[:, 0, :, :], b8[:, :, :], b8[:, :, 0:1].to_broadcast([P, FH, 8]),
                                      ALU.subtract).then_inc(best_ready, 1)
                    pos = p8[:, :, :].rearrange("p h k -> p (h k)")
                    step(dve.tensor_scalar(pij[:, 0, :], pos, 3, None, ALU.logical_shift_right))
                    step(dve.tensor_scalar(pij[:, 1, :], pos, 7, None, ALU.bitwise_and))
                    iota = iot[:, :].unsqueeze(1).to_broadcast([P, FH * 8, 8])
                    o3 = oneh[:, :, :, :].rearrange("p h k i -> p (h k) i")
                    for c in range(2):
                        step(dve.tensor_tensor(o3, pij[:, c, :].unsqueeze(2).to_broadcast([P, FH * 8, 8]), iota,
                                               ALU.is_equal))
                        step(dve.tensor_tensor(oneh[:, :, :, :], oneh[:, :, :, :],
                                               i8f[:, :, c, :].unsqueeze(2).to_broadcast([P, FH, 8, 8]), ALU.mult))
                        step(dve.tensor_reduce(picked[:, c, :], o3, AX_X, ALU.add))
                    dve.wait_ge(bexp_ready, g * 2 + a + 1)
                    step(dve.tensor_reduce(wsum[:, :], wsm[:, 1, :, :], AX_X, ALU.add))
                    step(dve.reciprocal(wsum[:, :], wsum[:, :]))
                    step(dve.tensor_tensor(wn[:, a, :].rearrange("p (h k) -> p h k", h=FH), wsm[:, 1, :, :],
                                           wsum[:, :].unsqueeze(2).to_broadcast([P, FH, 8]), ALU.mult))

                def write_idx(a):
                    dve.scalar_tensor_tensor(out=idx[a][:, :], in0=picked[:, 0, :], scalar=float(NE),
                                             in1=picked[:, 1, :], op0=ALU.mult, op1=ALU.add).then_inc(idx_ready, 1)

                if att:
                    dve.wait_ge(misc_ready, g * 24 + 1)
                    dve.tensor_scalar(work_f[:, 0:Q], MISC[:, 0:Q], cols[:, 0:1], None, ALU.add)\
                        .then_inc(misc_dve, 1)
                    dve.wait_ge(misc_dve, g * PER_MD + 1)
                    split(work_f[:, 0:Q], Q, step).then_inc(qparts_ready, 1)
                if fin:
                    gelu_val(7, g - 2)
                if ffn:
                    if fin:
                        dve.wait_ge(exp_dve, (g - 1) * EXP_DVE)
                        dve.wait_ge(val_ready, (g - 1) * NPAIR)
                    dve.wait_ge(x2_ready, g)
                    estep(g - 1, 1, dve.tensor_copy(x2c[:, :, :], x2n[:, :, :]))
                    estep(g - 1, 2, dve.tensor_copy(wc[:, :, :], wn[:, :, :]))
                if att:
                    for n in range(2 * NCH):
                        reduce(n, 0)
                    minus_max(0)
                if fin:
                    out_add(1, g - 2)
                if ffn:
                    if fin:
                        dve.wait_ge(out_ready, (g - 1) * 2)
                    estep(g - 1, 3, dve.tensor_copy(h1c[:, :, :], h1n[:, :, :]))
                for h in range(H):
                    rdone = ddone = 0
                    for q in range(NQ):
                        if att and h < H - 1:
                            for n in range(rdone, rdone + R_SPLIT[q]):
                                reduce(n, h + 1)
                            rdone += R_SPLIT[q]
                            if q == 5:
                                minus_max(h + 1)
                        if att and q == 2 and h:
                            norm_head(h - 1)
                        if ffn:
                            if q == 0 and h >= 3:
                                gelu_val(h - 3, g - 1)
                            if q == 1 and h == 7:
                                out_add(0, g - 1)
                            if h >= 2:
                                dots(h - 2, g - 1, ddone, DOT_SPLIT[q])
                                ddone += DOT_SPLIT[q]
                    if ffn and h >= 2:
                        gelu_arg(h - 2, g - 1)
                if att:
                    norm_head(H - 1)
                    dve.wait_ge(hres_in, (g + 1) * 16)
                    dve.wait_ge(misc_ready, g * 24 + 23)
                    dve.tensor_tensor(h1n[:, :, :], MISC[:, 0:Q].rearrange("p (a d) -> p a d", a=2), hres[:, :, :],
                                      ALU.add).then_inc(misc_dve, 1)
                    dve.wait_ge(misc_dve, (g + 1) * PER_MD)
                    for a in range(2):
                        last = dve.bn_stats(st[:, a, :], h1n[:, a, :])
                    last.then_inc(h1_ready, 1)
                    dve.wait_ge(h1_ready, g + 1)
                    settled(dve)
                    for a in range(2):
                        last = dve.bn_aggr(mv[:, a, :], st[:, a, :])
                    dve.wait_ge(att_dve, ta(last.then_inc(att_dve, 1)))
                    rsqrt(2, step)
                    for a in range(2):
                        last = dve.tensor_scalar(x2n[:, a, :], h1n[:, a, :], mv[:, a, 0:1], ln[:, 3, a:a + 1],
                                                 ALU.subtract, ALU.mult)
                    last.then_inc(x2_ready, 1)
                for a in range(2):
                    if ffn:
                        gelu_val(5 + a, g - 1)
                    if att:
                        select(a)
                        if a == 0:
                            write_idx(0)
                    if ffn:
                        dots(6 + a, g - 1, 0, PAIR)
                        gelu_arg(6 + a, g - 1)
                    if att and a == 1:
                        write_idx(1)
                if att:
                    ta.end()

            schedule(dve, setup, build, supertile)

        @block.tensor
        def _(pe):
            def place_parts(ps, c0, w, h, pattern):
                for j in range(len(pattern) // 2):
                    a, b = pattern[2 * j:2 * j + 2]
                    picks = [(E, a)] if a == b else [(2 * E, a), (0, b)]
                    for i, (at, part) in enumerate(picks):
                        last = pe.matmul(ps[32 * j:32 * j + 32, c0:c0 + w], selw[:, h, at:at + 2 * E], parts[:, part, 0:w],
                                         start=(i == 0), stop=(i == len(picks) - 1))
                return last

            def setup():
                pe.wait_ge(const_in, 16 * N_CONST)
                for n, tap in enumerate(TAP_ORDER):
                    terms = [(pp, s_, o) for pp, s_ in TAPS[tap] for o in range(2)]
                    for i, (pp, s_, o) in enumerate(terms):
                        pe.matmul(XB[n // 4][:, (n % 4) * D:(n % 4 + 1) * D], cw[:, o, s_ * C:(s_ + 1) * C],
                                  lw[:, 2 * pp + o, :], start=(i == 0), stop=(i == len(terms) - 1))
                for k in range(8):
                    last = pe.matmul(PV[:, 0:1], lw[:, k, :], cb[:, k % 2:k % 2 + 1], start=(k == 0), stop=(k == 7))
                last.then_inc(set_pe, 1)
                where = (bank[0], bank[1], UP, MISC)
                for h in range(FH):
                    for c in range(2):
                        r = slice(64 * c, 64 * c + 64)
                        last = pe.matmul(where[2 * c + h // 4][:, (h % 4) * NE:(h % 4 + 1) * NE], fq[r, h, :], fk[r, h, :],
                                         start=True, stop=True)
                last.then_inc(set_pe, 1)
                pe.wait_ge(set_act, 7)
                for h in range(FH):
                    for c in range(2):
                        r = slice(64 * c, 64 * c + 64)
                        last = pe.matmul(where[2 * c + h // 4][0:3, (h % 4) * NE:(h % 4 + 1) * NE], fb[r, h, :], fk[r, h, :],
                                         start=True, stop=True)
                last.then_inc(set_pe, 1)
                pe.wait_ge(set_dve, SETUP_DVE)

            def build(b):
                def tok(n):
                    pe.wait_ge(slab_in[n % 2], dma_count(b, n))
                    if n >= 2:
                        pe.wait_ge(tok_copied, b * (NTOKSTEP + 1) + n - 1)
                    ps = XB[n % 2][:, 0:TSTEP].rearrange("p (i j) -> p i j", j=NP)
                    for k, tap in enumerate(TAP_ORDER):
                        dy, dx = tap
                        i0 = 1 if (n == 0 and dy < 0) else 0
                        i1 = PROWS - 1 if (n == NTOKSTEP - 1 and dy > 1) else PROWS
                        j0, j1 = (1 if dx < 0 else 0), (NP - 1 if dx > 1 else NP)
                        r0, c0 = 2 * i0 + dy + 1, 2 * j0 + dx
                        last = pe.matmul(ps[:, i0:i1, j0:j1], w_tap[:, k, :],
                                         slab[n % 2][:, r0:r0 + 2 * (i1 - i0 - 1) + 1:2, c0:c0 + 2 * (j1 - j0 - 1) + 1:2],
                                         start=(k == 0), stop=(k == len(TAP_ORDER) - 1))
                    last.then_inc(tok_ready, 1)

                if first(b):
                    pe.wait_ge(set_act, 11)
                else:
                    pe.wait_ge(exp_done, b * SUP * PER_X)
                    pe.wait_ge(r_free, b * SUP * PER_R)
                    pe.wait_ge(ot_ready, b * SUP * H)
                    pe.wait_ge(misc_act, b * SUP * PER_MA)
                tok(0)
                tok(1)
                for c in range(NCH):
                    w, nt = CW[c], CT[c]
                    if c == NCH - 1:
                        pe.wait_ge(txt_in, (b + 1) * 16)
                        pe.wait_ge(xt_copied, b * NCH + c)
                        pe.transpose(XB[2][:, 0:P], txt_sb, idf[:, :]).then_inc(txt_ready, 1)
                    pe.wait_ge(tok_copied, b * (NTOKSTEP + 1) + (c + 2 if c < NCH - 1 else NTOKSTEP + 1))
                    if c >= 2:
                        pe.wait_ge(hrow_ready, b * NCH + c - 1)
                    for t in range(nt):
                        last = pe.transpose(RB[c % 2][:, t * P:(t + 1) * P], h_t[:, c * CH + t * P:c * CH + (t + 1) * P], idf[:, :])
                    last.then_inc(lnt_ready, 1)
                    if c + 2 < NTOKSTEP:
                        tok(c + 2)
                    pe.wait_ge(xrow_ready, b * NCH + c + 1)
                    if c:
                        pe.wait_ge(xt_copied, b * NCH + c)
                    for t in range(nt):
                        last = pe.transpose(XB[2][:, t * P:(t + 1) * P], xrow[:, c % 2, t, :], idf[:, :])
                    last.then_inc(xt_ready, 1)
                    pe.wait_ge(xt_copied, b * NCH + c + 1)
                    if c:
                        pe.wait_ge(place_dve, (b * NCH + c) * 4)
                        pe.wait_ge(place_act, (b * NCH + c) * 4)
                    pe.matmul(MISC[:, 0:w], wk_sb[:, :], h_t[:, c * CH:c * CH + w], start=True, stop=True).then_inc(k_ready, 1)
                    for t in range(nt):
                        m = min(P, w - t * P)
                        tok_cols = h_t[:, c * CH + t * P:c * CH + t * P + m]
                        pe.matmul(PV[0:m, t * P:(t + 1) * P], tok_cols, wv_sb[:, :], start=True, stop=False)
                        last = pe.matmul(PV[0:m, t * P:(t + 1) * P], ones3[:, 0:m], brow[:, FH * 2 * NE:FH * 2 * NE + D],
                                         start=False, stop=True)
                    last.then_inc(v_ready, 1)
                    pe.wait_ge(kparts_ready, b * NCH + c + 1)
                    pe.wait_ge(v_copied, b * (NCH + 1) + (c + 1 if c < NCH - 1 else NCH + 1))
                    for h in range(H):
                        if h >= 2:
                            if h % 2 == 0:
                                pe.wait_ge(place_dve, (b * NCH + c) * 4 + h // 2)
                            else:
                                pe.wait_ge(place_act, (b * NCH + c) * 4 + h // 2)
                        last = place_parts(MISC if h % 2 == 0 else PV, 0, w, h, KPART)
                        last.then_inc(place_ready, 1)
                pe.wait_ge(place_dve, (b + 1) * NCH * 4)
                pe.wait_ge(place_act, (b + 1) * NCH * 4)

            def supertile(g, s, att, ffn, fin):
                def ups(j, f, k0, n):
                    for k in range(k0, k0 + n):
                        u = j * PAIR + k
                        if u % 64 == 0:
                            if u:
                                pe.wait_ge(out_ready, f * 2 + 1)
                            elif not (isinstance(f, int) and f == 0):
                                pe.wait_ge(out_ready, f * 2)
                        pe.wait_ge(diag_ready, f * PER_UP + u + 1)
                        pe.matmul(UP[:, 0:D], diag[:, u % 8, :], gat[:, (j % RING) * PAIR + k, D:2 * D],
                                  start=(u % 64 == 0), stop=(u % 64 == 63)).then_inc(up_done, 1)

                def row_chunk(n, h):
                    a, c = n // NCH, n % NCH
                    k = h * 2 * NCH + n
                    if not (isinstance(g, int) and g == 0 and k < 2):
                        pe.wait_ge(r_free, g * PER_R + k - 1)
                    pe.matmul(RB[k % 2][:, 0:CW[c]], qst[0:SROWS, h, a * P:(a + 1) * P], kst[0:SROWS, h, c * CH:c * CH + CW[c]],
                              start=True, stop=True).then_inc(r_ready, 1)

                def turn_max(h):
                    pe.wait_ge(mneg_ready, g * H + h + 1)
                    if h < 2:
                        pe.wait_ge(misc_act, g * PER_MA + 4 + h)
                    else:
                        pe.wait_ge(misc_dve, g * PER_MD + h)
                    for a in range(2):
                        last = pe.matmul(MISC[SHIFT:P, a * P:(a + 1) * P], mneg[:, a, :], idb[:, :], start=True, stop=True)
                    last.then_inc(misc_ready, 1)

                def turn_out(h):
                    pe.wait_ge(ot_ready, g * H + h + 1)
                    if h < H - 1:
                        pe.wait_ge(misc_act, g * PER_MA + 6 + h)
                    else:
                        pe.wait_ge(misc_dve, g * PER_MD + H)
                    for a in range(2):
                        last = pe.matmul(MISC[:, 17 * a:17 * a + 17], o_t[:, a * P:(a + 1) * P], selv[:, :], start=True, stop=True)
                    last.then_inc(misc_ready, 1)

                def weigh(h, q):
                    t0, nt = QUADS[q]
                    if q == 0 and not (isinstance(g, int) and g == 0 and h == 0):
                        pe.wait_ge(ot_ready, g * H + h)
                    for i in range(nt):
                        t = t0 + i
                        n = h * XCH + t // 2
                        if i % 2 == 0:
                            pe.wait_ge(exp_done, g * PER_X + n + 1)
                        v0 = (t * H + h) * 17
                        last = pe.matmul(PV[32 * i:32 * i + 32, 0:Q], vals_sb[:, v0:v0 + 32],
                                         probs[:, n % 4, (t % 2) * Q:(t % 2 + 1) * Q], start=(t < 4), stop=(t + 4 >= NT))
                        if i % 2:
                            last.then_inc(pv_done, 1)

                if att:
                    if not (isinstance(g, int) and g == 0):
                        pe.wait_ge(misc_act, g * PER_MA)
                    pe.matmul(MISC[:, 0:Q], wq_sb[:, :], h_t[:, bass.ds(s * Q, Q)], start=True, stop=True).then_inc(misc_ready, 1)
                    pe.wait_ge(qparts_ready, g + 1)
                    for u in range(4):
                        if u:
                            pe.wait_ge(misc_act, g * PER_MA + u)
                        for i in range(2):
                            last = place_parts(MISC, i * Q, Q, 2 * u + i, QPART)
                        last.then_inc(misc_ready, 1)
                    pe.wait_ge(misc_act, g * PER_MA + 4)
                    for n in range(2 * NCH):
                        row_chunk(n, 0)
                    turn_max(0)
                if fin:
                    ups(7, g - 2, 0, PAIR)
                for h in range(H):
                    if att:
                        pe.wait_ge(misc_act, g * PER_MA + 5 + h)
                    rdone = udone = 0
                    for q, (t0, nt) in enumerate(QUADS):
                        if att:
                            for i in range(nt // 2):
                                n = h * XCH + t0 // 2 + i
                                if n >= 3:
                                    pe.wait_ge(exp_done, g * PER_X + n - 2)
                                elif not (isinstance(g, int) and g == 0):
                                    pe.wait_ge(exp_done, g * PER_X)
                                for k in range(2):
                                    t = t0 + 2 * i + k
                                    last = pe.matmul(XB[n % 3][:, k * Q:(k + 1) * Q], kst[:, h, t * P:(t + 1) * P], qst[:, h, :],
                                                     start=True, stop=True)
                                last.then_inc(x_ready, 1)
                            if h < H - 1:
                                for n in range(rdone, rdone + R_SPLIT[q]):
                                    row_chunk(n, h + 1)
                                rdone += R_SPLIT[q]
                            if q == 2 and h:
                                turn_out(h - 1)
                            if q:
                                weigh(h, q - 1)
                            if q == 6 and h < H - 1:
                                turn_max(h + 1)
                        if ffn and h >= 3:
                            ups(h - 3, g - 1, udone, UP_SPLIT[q])
                            udone += UP_SPLIT[q]
                    if att:
                        weigh(h, NQ - 1)
                if att:
                    turn_out(H - 1)
                    pe.wait_ge(misc_dve, g * PER_MD + H + 1)
                    for a in range(2):
                        last = pe.transpose(MISC[:, a * P:(a + 1) * P], o_n[:, a, :], idf[:, :])
                    last.then_inc(misc_ready, 1)
                    pe.wait_ge(misc_act, g * PER_MA + 13)
                    for a in range(2):
                        pe.matmul(MISC[:, a * P:(a + 1) * P], c_t[:, a * P:(a + 1) * P], wo_sb[:, :], start=True, stop=False)
                        last = pe.matmul(MISC[:, a * P:(a + 1) * P], ones3[:, :], brow[:, FH * 2 * NE + D:], start=False, stop=True)
                    last.then_inc(misc_ready, 1)
                    pe.wait_ge(x2_ready, g + 1)
                    for a in range(2):
                        last = pe.transpose(MISC[:, a * P:(a + 1) * P], x2n[:, a, :], idf[:, :])
                    last.then_inc(misc_ready, 1)
                    pe.wait_ge(misc_act, (g + 1) * PER_MA)
                for a in range(2):
                    if att:
                        for c4 in range(4):
                            k = H * 2 * NCH + 4 * a + c4
                            pe.wait_ge(r_free, g * PER_R + k - 1)
                            pe.matmul(RB[k % 2][:, :], x2t[:, a * P:(a + 1) * P], w_s[:, c4 * 512:(c4 + 1) * 512], start=True, stop=False)
                            pe.matmul(RB[k % 2][:, :], ones3[:, :], brow[:, c4 * 512:(c4 + 1) * 512], start=False, stop=True)\
                                .then_inc(r_ready, 1)
                    if ffn:
                        ups(5 + a, g - 1, 0, PAIR)

            schedule(pe, setup, build, supertile)


def kernel(x, txt, L0_tok_conv_w, L0_tok_conv_b, L0_tok_lin_w, L0_tok_lin_b, L0_attn_Wq, L0_attn_Wk, L0_attn_Wv,
           L0_attn_bq, L0_attn_bk, L0_attn_bv, L0_attn_Wo, L0_attn_bo, L0_ffn_Wq, L0_ffn_bq, L0_ffn_keys,
           L0_ffn_w_down_embed, L0_ffn_w_up_embed):
    import numpy as np
    import concourse.bacc as bacc
    from concourse.bass_utils import run_bass_kernel_spmd

    def by_head(w):
        return np.transpose(np.asarray(w), (1, 0, 2)).reshape(D, D)

    sel_w = np.zeros((H, E, H, 4, E), np.float32)
    for h in range(H):
        for e in range(E):
            sel_w[h, e, h, 1:3, e] = 1

    sel_v = np.zeros((P, 17), np.float32)
    for group in range(4):
        sel_v[32 * group + np.arange(17), np.arange(17)] = 1
    bv, bo = np.asarray(L0_attn_bv).reshape(D), np.asarray(L0_attn_bo)
    arrays = {
        "x": x, "txt": txt, "conv_w": L0_tok_conv_w, "conv_b": np.asarray(L0_tok_conv_b).reshape(2, P).T,
        "lin_wt": np.asarray(L0_tok_lin_w).T, "lin_b": np.asarray(L0_tok_lin_b).reshape(D, 1),
        "wq": by_head(L0_attn_Wq), "wk": by_head(L0_attn_Wk), "wv": by_head(L0_attn_Wv),
        "bq": np.asarray(L0_attn_bq).reshape(D, 1), "bk": np.asarray(L0_attn_bk).reshape(D, 1),
        "bvo": np.stack([np.concatenate([bv, bo])] * 3), "wo": L0_attn_Wo,
        "ffn_wq": L0_ffn_Wq, "ffn_bq": np.stack([np.asarray(L0_ffn_bq)] * 3, axis=1),
        "ffn_keys_t": np.transpose(np.asarray(L0_ffn_keys), (1, 3, 0, 2)),
        "table": np.concatenate([np.asarray(L0_ffn_w_down_embed), np.asarray(L0_ffn_w_up_embed)], axis=1),
        "ident": np.eye(P, dtype=np.float32), "sel_w": sel_w.reshape(P, -1), "sel_v": sel_v,
        "part_masks": np.array([[0, 0], [1, 0], [1, 1]], np.float32),
        "iota8": np.stack([np.arange(8, dtype=np.float32)] * P),
    }
    nc = bacc.Bacc("TRN2", target_bir_lowering=False, num_devices=1)
    in_map, args = {}, []
    for name, a in arrays.items():
        a = np.ascontiguousarray(a)
        in_map[f"in_{name}"] = a
        args.append(nc.dram_tensor(f"in_{name}", a.shape, mybir.dt.from_np(a.dtype), kind="ExternalInput").ap())
    args.append(nc.dram_tensor("out_rows", (B * NPAD, D), F32, kind="ExternalOutput").ap())
    early_fusion(nc, *args)
    r = run_bass_kernel_spmd(nc, [in_map], core_ids=[0])
    return r.results[0]["out_rows"].reshape(B, NPAD, D)[:, :NTOK, :]
```

```python
from contextlib import ExitStack

import concourse.bass as bass
from concourse import mybir

F32 = mybir.dt.float32
BF16 = mybir.dt.bfloat16
U32 = mybir.dt.uint32
ACT = mybir.ActivationFunctionType
ALU = mybir.AluOpType
AX_X = mybir.AxisListType.X

P = 128
B, C, IMG = 4, 128, 112
D = 128
H, E = 8, 16
NP = IMG // 2
NTXT = 128
NTOK = NP * NP + NTXT
NT = -(-NTOK // P)
NPAD = NT * P
Q = 256
SUP = NPAD // Q
G_ALL = B * SUP
FH, TOPK, NE = 8, 8, 128
EPS = 1e-5

KPART = (0, 0, 1, 1, 0, 2)
QPART = (0, 1, 0, 1, 2, 0)
SROWS = len(KPART) * E
SHIFT = SROWS

SHIFTS = ((0, 0), (0, -1), (0, 1), (-1, 0), (1, 0))
TAPS = {}
for _py in range(2):
    for _px in range(2):
        for _s, (_dy, _dx) in enumerate(SHIFTS):
            TAPS.setdefault((_py + _dy, _px + _dx), []).append((_py * 2 + _px, _s))
TAP_ORDER = sorted(TAPS, key=lambda t: (t[0] not in (0, 1)) or (t[1] not in (0, 1)))

PROWS = 8
NTOKSTEP = NP // PROWS
TSTEP = PROWS * NP
CH = 512
NCH = -(-NTOK // CH)
CW = [min(CH, NTOK - c * CH) for c in range(NCH)]
CT = [-(-w // P) for w in CW]
QUADS = [(q * 4, min(4, NT - q * 4)) for q in range(-(-NT // 4))]
NQ = len(QUADS)
XCH = NT // 2

PER_R = H * 2 * NCH + 2 * 4
PER_X = H * XCH
PER_MA, PER_MD = 10, 9
PER_M = PER_MA + PER_MD
PAIR = 16
NPAIR = 2 * FH * TOPK // PAIR
PER_UP = NPAIR * PAIR
RING = 4
R_AT = (2, 2, 1, 2, 1, 1, 2, 1, 1, 1, 0, 0, 0)
R_AT0 = (0, 0, 0, 0, 3, 3, 2, 2, 2, 2, 0, 0, 0)
D_AT = (0, 0, 1, 0, 1, 2, 0, 2, 2, 2, 0, 3, 3)
DIAG_AT = (0, 0, 0, 2, 2, 1, 2, 1, 2, 1, 2, 1, 2)
UP_AT = (0, 0, 0, 0, 0, 2, 1, 2, 1, 2, 2, 1, 1)
UP_LATE = (2, 2, 0, 0, 0, 0, 0, 0, 0, 0, 0, 0, 0)
assert sum(R_AT) == sum(R_AT0) == 2 * NCH and sum(D_AT) == sum(DIAG_AT) == sum(UP_AT) + sum(UP_LATE) == PAIR
GELU_C = 2.0 * 0.7978845608028654
RSQRT_SEED = float(0x5F3759DF)
PAIR_DVE = PAIR + 5
EXP_DVE = 2 + NPAIR * PAIR_DVE
SETUP_DVE = 18
BUILD_DVE = 140
ATT_DVE = 52
PREP_DVE = 8
SEL_DVE = 19


def first(b):
    return isinstance(b, int) and b == 0


def misc_m(h):
    return 1 if h == 0 else 2 * h


def misc_o(h):
    return 2 * h + 3 if h < H - 1 else 2 * H


def row_base(g, h, carried):
    return g * PER_R + h * 2 * NCH - (8 if carried and h == 0 else 0)


def sub_base(g, a, carried):
    return (g + 1) * PER_R - 8 + 4 * a + (2 * NCH if carried else 0)


def dma_count(b, n, per=(NTOKSTEP + 1) // 2, other=NTOKSTEP // 2):
    return 16 * (b * (per if n % 2 == 0 else other) + n // 2 + 1)


class Tally:

    def __init__(self, per):
        self.per, self.base, self.k = per, 0, 0

    def begin(self, index):
        self.base, self.k = index * self.per, 0

    def __call__(self, instruction):
        self.k += 1
        return self.base + self.k

    def end(self):
        assert self.k == self.per, (self.k, self.per)


def early_fusion(nc, x, txt, conv_w, conv_b, lin_wt, lin_b, wq, wk, wv, bq, bk, bvo, wo,
                 ffn_wq, ffn_bq, ffn_keys_t, table, ident, sel_w, sel_v, part_masks, iota8, out):
    with ExitStack() as ctx:
        def sb(name, shape, dt):
            return ctx.enter_context(nc.sbuf_tensor(name, shape, dt))

        def sem(name):
            return ctx.enter_context(nc.semaphore(name))

        kst = sb("key_stack", [P, H, NPAD], BF16)
        vals_sb = sb("values", [P, NT * H * 17 + 15], F32)
        v4 = vals_sb[:, 0:NT * H * 17].rearrange("p (t h c) -> p t h c", t=NT, c=17)
        h_t = sb("h_t", [P, NPAD], F32)
        gat = sb("gathered", [P, RING * PAIR, 2 * D], F32)
        qst = sb("query_stack", [P, H, Q], BF16)
        xrow = (qst[:, :, :].rearrange("p h q -> p (h q)").bitcast(F32)
                .rearrange("p (c t d) -> p c t d", c=2, t=4))
        probs = sb("probs", [P, 4, 2 * Q], F32)
        diag = sb("diag", [P, 8, D], F32)
        hrow = diag[:, :, :].rearrange("p (c t) d -> p c t d", c=2)
        slab = [sb(f"slab{i}", [P, 2 * PROWS + 2, IMG], F32) for i in range(1)]
        slab.append(probs[:, :, :].rearrange("p a b -> p (a b)")[:, 0:(2 * PROWS + 2) * IMG]
                    .rearrange("p (r w) -> p r w", w=IMG))
        w_tap = sb("w_tap", [P, 12, D], F32)
        w_s = sb("w_s", [P, FH * 2 * NE], F32)
        wq_sb = sb("wq_sb", [P, D], F32)
        wk_sb = sb("wk_sb", [P, D], F32)
        wv_sb = sb("wv_sb", [P, D], F32)
        wo_sb = sb("wo_sb", [P, D], F32)
        cols = sb("cols", [P, 4], F32)
        brow = sb("brow", [3, FH * 2 * NE + 2 * D], BF16)
        idf = sb("idf", [P, P], F32)
        idb = sb("idb", [P, P], BF16)
        selw = sb("selw", [P, H, 4 * E], BF16)
        selv = sb("selv", [P, 17], F32)
        masks = sb("masks", [3, 2], F32)
        iot = sb("iot", [P, 8], F32)
        ones3 = sb("ones3", [3, P], BF16)
        shared = sb("shared", [P, 3 * CH // 2], F32)
        parts = shared[:, :].bitcast(BF16).rearrange("p (a n) -> p a n", a=3)
        o_n = shared[:, 0:2 * D].rearrange("p (a d) -> p a d", a=2)
        qparts = probs[:, 0, 0:3 * Q // 2].bitcast(BF16).rearrange("p (a n) -> p a n", a=3)
        c_t = shared[:, 2 * D:2 * D + Q]
        s8 = shared[:, 512:640].rearrange("p (h c k) -> p h c k", h=FH, c=2)
        i8 = shared[:, 640:768].bitcast(U32).rearrange("p (h c k) -> p h c k", h=FH, c=2)
        st = sb("st", [P, 4, 6], F32)
        mv = sb("mv", [P, 4, 2], F32)
        ln = sb("ln", [P, 6, 4], F32)
        lnu = sb("lnu", [P, 2, 4], U32)
        hres = sb("hres", [P, 2, D], F32)
        mxp = sb("mxp", [P, 2, NCH], F32)
        mx = sb("mx", [P, 2, 2], F32)
        mneg = sb("mneg", [P, 2, 32], BF16)
        o_t = sb("o_t", [P, Q], F32)
        rcp = sb("rcp", [P, 2, 1], F32)
        h1n = sb("h1n", [P, 2, D], F32)
        h1c = sb("h1c", [P, 2, D], F32)
        x2n = sb("x2n", [P, 2, D], F32)
        x2c = sb("x2c", [P, 2, D], F32)
        x2t = c_t
        i8f = sb("i8f", [P, FH, 2, 8], F32)
        b8 = sb("b8", [P, FH, 8], F32)
        p8 = sb("p8", [P, FH, 8], U32)
        pij = sb("pij", [P, 2, FH * 8], U32)
        oneh = sb("oneh", [P, FH, 8, 8], F32)
        work_f = oneh[:, :, :, :].rearrange("p h k i -> p (h k i)")
        picked = sb("picked", [P, 2, FH * 8], F32)
        wsm = sb("wsm", [P, 2, FH, 8], F32)
        wsum = sb("wsum", [P, FH], F32)
        wn = sb("wn", [P, 2, FH * 8], F32)
        idx = [sb(f"idx{a}", [P, FH * 8], U32) for a in range(2)]
        xd = sb("xd", [P, PAIR], F32)
        gz = sb("gz", [P, 4, PAIR], F32)
        ge = sb("ge", [P, PAIR], F32)
        gv = sb("gv", [P, 2, PAIR], F32)
        ostage = sb("ostage", [P, 2, D], F32)
        txt_sb = o_t[:, 0:D]

        gflat = gat[:, :, :].rearrange("p a b -> p (a b)")
        cw = gflat[:, 0:1280].rearrange("p (o n) -> p o n", o=2)
        lw = gflat[:, 1280:2304].rearrange("p (k d) -> p k d", k=8)
        fq = gflat[:, 2304:3328].rearrange("p (h d) -> p h d", h=FH)
        fk = gflat[:, 3328:4352].rearrange("p (h e) -> p h e", h=FH)
        fb = gflat[:, 4352:4376].rearrange("p (h r) -> p h r", h=FH)
        cb = gflat[:, 4376:4378]
        NB = FH * 2 * NE + 2 * D
        brf = gflat[0:3, 4400:4400 + NB]
        brt = gflat[0:3, 6800:6800 + NB]
        selw_f = gflat[:, 9200:9200 + H * 4 * E]
        brh = gflat[0:3, 14000:14000 + NB // 2].bitcast(BF16)

        bank = [ctx.enter_context(nc.psum_tensor(f"bank{i}", [P, 512], F32)) for i in range(8)]
        RB, XB, PV, UP, MISC = bank[0:2], bank[2:5], bank[5], bank[6], bank[7]

        h_dram = nc.dram_tensor("h_rows", [B * NPAD, D], F32, kind="Internal").ap()

        const_in = sem("const_in")
        table_in = sem("table_in")
        set_pe = sem("set_pe")
        set_act = sem("set_act")
        set_dve = sem("set_dve")
        slab_in = [sem("slab_in0"), sem("slab_in1")]
        txt_in = sem("txt_in")
        txt_ready = sem("txt_ready")
        tok_ready = sem("tok_ready")
        tok_copied = sem("tok_copied")
        lnt_ready = sem("lnt_ready")
        hrow_ready = sem("hrow_ready")
        hrow_stored = [sem("hrow_stored0"), sem("hrow_stored1")]
        xrow_ready = sem("xrow_ready")
        xt_ready = sem("xt_ready")
        xt_copied = sem("xt_copied")
        k_ready = sem("k_ready")
        kf_ready = sem("kf_ready")
        kparts_ready = sem("kparts_ready")
        v_ready = sem("v_ready")
        v_copied = sem("v_copied")
        place_ready = sem("place_ready")
        place_dve = sem("place_dve")
        place_act = sem("place_act")
        build_dve = sem("build_dve")
        hres_in = sem("hres_in")
        misc_ready = sem("misc_ready")
        misc_act = sem("misc_act")
        misc_dve = sem("misc_dve")
        qp_ready = sem("qp_ready")
        qparts_ready = sem("qparts_ready")
        qp_act = sem("qp_act")
        prep_dve = sem("prep_dve")
        sel_dve = sem("sel_dve")
        r_ready = sem("r_ready")
        r_free = sem("r_free")
        mneg_ready = sem("mneg_ready")
        x_ready = sem("x_ready")
        exp_done = sem("exp_done")
        pv_done = sem("pv_done")
        ot_ready = sem("ot_ready")
        o_ready = sem("o_ready")
        x2_ready = sem("x2_ready")
        h1_ready = sem("h1_ready")
        best_ready = sem("best_ready")
        bexp_ready = sem("bexp_ready")
        att_dve = sem("att_dve")
        idx_ready = sem("idx_ready")
        rows_in = [sem(f"rows_in{i}") for i in range(2 * RING)]
        z_ready = sem("z_ready")
        e_ready = sem("e_ready")
        val_ready = sem("val_ready")
        diag_ready = sem("diag_ready")
        up_done = sem("up_done")
        out_ready = sem("out_ready")
        out_stored = [sem("out_stored0"), sem("out_stored1")]
        exp_dve = sem("exp_dve")

        N_CONST = 19

        def schedule(eng, setup, build, supertile):
            setup()
            build(0)
            supertile(0, 0, True, False, False, True)
            supertile(1, 1, True, True, True, True)
            with eng.Fori(2, SUP - 1) as s:
                supertile(s, s, True, True, True, True)
            supertile(SUP - 1, SUP - 1, True, True, True, False)
            with eng.Fori(1, B) as b:
                build(b)
                supertile(b * SUP, 0, True, True, False, True)
                with eng.Fori(1, SUP - 1) as s:
                    supertile(b * SUP + s, s, True, True, True, True)
                supertile(b * SUP + SUP - 1, SUP - 1, True, True, True, False)
            supertile(G_ALL, None, False, True, False, False)

        passed = {nc.vector: sem("passed_dve"), nc.gpsimd: sem("passed_pool"), nc.sync: sem("passed_sp")}

        def settled(eng):
            eng.sem_inc(passed[eng], 1)

        block = ctx.enter_context(nc.Block())

        @block.sync
        def _(sp):
            def setup():
                pairs = [
                    (cw, conv_w.rearrange("(o p) n -> p o n", p=P)),
                    (lw, lin_wt.rearrange("(k p) d -> p k d", p=P)),
                    (cb, conv_b),
                    (fq, ffn_wq.rearrange("(h p) d -> p h d", p=P)),
                    (fk, ffn_keys_t.rearrange("c f h e -> (c f) h e")),
                    (fb, ffn_bq.rearrange("(h p) r -> p h r", p=P)),
                    (wq_sb[:, :], wq), (wk_sb[:, :], wk), (wv_sb[:, :], wv), (wo_sb[:, :], wo),
                    (cols[:, 0:1], bq), (cols[:, 1:2], bk), (cols[:, 3:4], lin_b),
                    (brf[:, FH * 2 * NE:], bvo),
                    (idf[:, :], ident),
                    (selw_f, sel_w), (selv[:, :], sel_v),
                    (masks[:, :], part_masks), (iot[:, :], iota8),
                ]
                assert len(pairs) == N_CONST, len(pairs)
                for dst, src in pairs:
                    sp.dma_start(dst, src).then_inc(const_in, 16)

            def build(b):
                def load_slab(n):
                    i = n % 2
                    if n >= 2:
                        sp.wait_ge(tok_ready, b * NTOKSTEP + n - 1)
                    elif not first(b):
                        sp.wait_ge(tok_ready, b * NTOKSTEP)
                        sp.wait_ge(pv_done, b * SUP * PER_X)
                    lo, hi = max(0, 2 * PROWS * n - 1), min(IMG, 2 * PROWS * (n + 1) + 1)
                    at = 1 if n == 0 else 0
                    sp.dma_start(slab[i][:, at:at + hi - lo, :],
                                 x[bass.ds(b, 1), :, lo:hi, :].rearrange("b c r w -> (b c) r w")).then_inc(slab_in[i], 16)

                load_slab(0)
                load_slab(1)
                if not first(b):
                    sp.wait_ge(misc_ready, b * SUP * PER_M)
                sp.dma_start(txt_sb, txt[bass.ds(b, 1), :, :].rearrange("b t d -> (b t) d")).then_inc(txt_in, 16)
                for c in range(NCH):
                    if c + 2 < NTOKSTEP:
                        load_slab(c + 2)
                    sp.wait_ge(hrow_ready, b * NCH + c + 1)
                    rows = h_dram[bass.ds(b * NPAD + c * CH, CT[c] * P), :]
                    sp.dma_start(rows.rearrange("(t p) d -> p t d", p=P), hrow[:, c % 2, 0:CT[c], :])\
                        .then_inc(hrow_stored[c % 2], 16)
                sp.wait_ge(hrow_stored[0], dma_count(b, NCH - 1))
                sp.wait_ge(hrow_stored[1], dma_count(b, NCH - 2))
                settled(sp)

            def supertile(g, s, att, ffn, taken, ahead):
                if att:
                    if not (isinstance(g, int) and g == 0):
                        sp.wait_ge(h1_ready, g)
                    sp.dma_start(hres[:, :, :], h_dram[bass.ds(g * Q, Q), :].rearrange("(t p) d -> p t d", p=P))\
                        .then_inc(hres_in, 16)
                if ffn:
                    for a in range(2):
                        sp.wait_ge(out_ready, (g - 1) * 2 + a + 1)
                        sp.dma_start(out[bass.ds((g - 1) * Q + a * P, P), :], ostage[:, a, :]).then_inc(out_stored[a], 16)

            schedule(sp, setup, build, supertile)
            for o in out_stored:
                sp.wait_ge(o, 16 * G_ALL)

        @block.gpsimd
        def _(pool):
            def gather(f, first_f):
                for j in range(NPAIR):
                    a = j // 4
                    if j % 4 == 0:
                        pool.wait_ge(idx_ready, f * 2 + a + 1)
                    if not (first_f and j < RING):
                        pool.wait_ge(up_done, f * PER_UP + (j - RING + 1) * PAIR)
                    settled(pool)
                    for k in range(PAIR):
                        col = (j % 4) * PAIR + k
                        pool.indirect_dma_start(
                            gat[:, (j % RING) * PAIR + k, :], None, table,
                            bass.IndirectOffsetOnAxis(ap=idx[a][:, col:col + 1], axis=0),
                        ).then_inc(rows_in[2 * (j % RING) + k // 8], 16)

            gather(0, True)
            with pool.Fori(1, G_ALL) as f:
                gather(f, False)

        @block.scalar
        def _(act):
            def setup():
                act.wait_ge(set_pe, 1)
                for i in range(3):
                    act.activation(w_tap[:, 4 * i:4 * i + 4, :], XB[i][:, :].rearrange("p (t d) -> p t d", d=D),
                                   ACT.Copy).then_inc(set_act, 1)
                act.wait_ge(set_pe, 2)
                ws4 = w_s[:, :].rearrange("p (h c e) -> p h c e", h=FH, c=2)
                for i, bk_ in enumerate((bank[0], bank[1], UP, MISC)):
                    c, hh = i // 2, i % 2
                    act.activation(ws4[:, 4 * hh:4 * hh + 4, c, :], bk_[:, :].rearrange("p (h e) -> p h e", e=NE),
                                   ACT.Copy).then_inc(set_act, 1)
                act.wait_ge(set_pe, 3)
                bs4 = brf[:, 0:FH * 2 * NE].rearrange("p (h c e) -> p h c e", h=FH, c=2)
                for i, bk_ in enumerate((bank[0], bank[1], UP, MISC)):
                    c, hh = i // 2, i % 2
                    act.activation(bs4[:, 4 * hh:4 * hh + 4, c, :], bk_[0:3, :].rearrange("p (h e) -> p h e", e=NE),
                                   ACT.Copy).then_inc(set_act, 1)

            def build(b):
                def tok(n):
                    act.wait_ge(tok_ready, b * NTOKSTEP + n + 1)
                    act.activation(h_t[:, n * TSTEP:(n + 1) * TSTEP], XB[n % 2][:, 0:TSTEP], ACT.Identity,
                                   bias=cols[:, 2:3]).then_inc(tok_copied, 1)

                if first(b):
                    act.wait_ge(set_dve, SETUP_DVE)
                tok(0)
                tok(1)
                for c in range(NCH):
                    w, nt = CW[c], CT[c]
                    if c == NCH - 1:
                        act.wait_ge(txt_ready, b + 1)
                        act.activation(h_t[:, NP * NP:NTOK], XB[2][:, 0:P], ACT.Copy).then_inc(tok_copied, 1)
                    act.wait_ge(lnt_ready, b * NCH + c + 1)
                    if c >= 2:
                        act.wait_ge(hrow_stored[c % 2], dma_count(b, c - 2))
                        act.wait_ge(xrow_ready, b * NCH + c - 1)
                    elif not first(b):
                        act.wait_ge(hrow_stored[c % 2], dma_count(b, c) - 16)
                    act.activation(hrow[:, c % 2, 0:nt, :], RB[c % 2][:, 0:nt * P].rearrange("p (t d) -> p t d", d=D),
                                   ACT.Copy).then_inc(hrow_ready, 1)
                    if c + 2 < NTOKSTEP:
                        tok(c + 2)
                    act.wait_ge(xt_ready, b * NCH + c + 1)
                    act.activation(h_t[:, c * CH:c * CH + nt * P], XB[2][:, 0:nt * P], ACT.Copy).then_inc(xt_copied, 1)
                    act.wait_ge(k_ready, b * NCH + c + 1)
                    if c or not first(b):
                        act.wait_ge(kparts_ready, b * NCH + c)
                    act.activation(work_f[:, 0:w], MISC[:, 0:w], ACT.Identity, bias=cols[:, 1:2]).then_inc(kf_ready, 1)
                    act.wait_ge(v_ready, b * NCH + c + 1)
                    full = w // P
                    last = act.activation(v4[:, 4 * c:4 * c + full, :, 0:E],
                                          PV[:, 0:full * P].rearrange("p (t h e) -> p t h e", t=full, e=E), ACT.Copy)
                    if w % P:
                        r = w % P
                        last.then_inc(v_copied, 1)
                        last = act.activation(v4[0:r, 4 * c + full, :, 0:E],
                                              PV[0:r, full * P:(full + 1) * P].rearrange("p (h e) -> p h e", e=E), ACT.Copy)
                    last.then_inc(v_copied, 1)
                    for h in range(1, H, 2):
                        act.wait_ge(place_ready, (b * NCH + c) * H + h + 1)
                        act.activation(kst[0:SROWS, h, c * CH:c * CH + w], PV[0:SROWS, 0:w], ACT.Copy)\
                            .then_inc(place_act, 1)
                act.wait_ge(hrow_stored[0], dma_count(b, NCH - 1))
                act.wait_ge(hrow_stored[1], dma_count(b, NCH - 2))

            def supertile(g, s, att, ffn, taken, ahead):
                f = g - 1

                def gexp(j):
                    act.wait_ge(z_ready, f * NPAIR + j + 1)
                    act.activation(ge[:, :], gz[:, 2, :], ACT.Exp, scale=-GELU_C).then_inc(e_ready, 1)

                def diags(j, i0, n):
                    for k in range(i0, i0 + n):
                        if k == 0:
                            act.wait_ge(val_ready, f * NPAIR + j + 1)
                        u = j * PAIR + k
                        if not (isinstance(f, int) and f == 0 and u < 8):
                            act.wait_ge(up_done, f * PER_UP + u - 7)
                        act.activation(diag[:, u % 8, :], idf[:, :], ACT.Copy, scale=gv[:, j % 2, k:k + 1])\
                            .then_inc(diag_ready, 1)

                def place_q(n, u):
                    act.wait_ge(qp_ready, n * 5 + 2 + u)
                    act.activation(qst[0:SROWS, 2 * u:2 * u + 2, :],
                                   XB[(u + 1) % 3][0:SROWS, :].rearrange("p (h q) -> p h q", q=Q), ACT.Copy)\
                        .then_inc(qp_act, 1)

                def place_max(n, h):
                    act.wait_ge(misc_ready, n * PER_M + misc_m(h))
                    act.activation(qst[SHIFT:P, h, :], MISC[SHIFT:P, 0:Q], ACT.Copy).then_inc(misc_act, 1)

                def head_out(h):
                    act.wait_ge(pv_done, g * PER_X + (h + 1) * XCH)
                    if h:
                        act.wait_ge(misc_ready, g * PER_M + misc_o(h - 1))
                    act.activation(o_t[:, :], PV[:, 0:Q], ACT.Copy).then_inc(ot_ready, 1)

                def best_exp(n, a):
                    act.wait_ge(best_ready, n * 2 + a + 1)
                    act.activation(wsm[:, 1, :, :], wsm[:, 0, :, :], ACT.Exp).then_inc(bexp_ready, 1)

                if att and not taken:
                    for u in range(4):
                        place_q(g, u)
                    place_max(g, 0)
                for h in range(H):
                    j = h - 2
                    done = 0
                    for p in range(XCH):
                        if att:
                            n = h * XCH + p
                            act.wait_ge(x_ready, g * PER_X + n + 1)
                            if not (isinstance(g, int) and g == 0 and n < 4):
                                act.wait_ge(pv_done, g * PER_X + n - 3)
                            act.activation(probs[:, n % 4, :], XB[n % 3][:, :], ACT.Exp, scale=E ** -0.5)\
                                .then_inc(exp_done, 1)
                            if h and p == 1:
                                head_out(h - 1)
                            if taken and h == 0 and p == 4:
                                best_exp(g - 1, 1)
                            if h < H - 1 and p == 11:
                                place_max(g, h + 1)
                        if ffn and j >= 0:
                            if p == 0:
                                gexp(j)
                            diags(j, done, DIAG_AT[p])
                            done += DIAG_AT[p]
                if att:
                    head_out(H - 1)
                if ffn:
                    gexp(6)
                if att:
                    act.wait_ge(misc_ready, g * PER_M + 17)
                    act.activation(c_t, MISC[:, 0:Q], ACT.Copy).then_inc(misc_act, 1)
                if ahead:
                    for u in range(4):
                        place_q(g + 1, u)
                if ffn:
                    diags(6, 0, 8)
                if att:
                    act.wait_ge(misc_ready, g * PER_M + 19)
                    act.activation(x2t, MISC[:, 0:Q], ACT.Copy).then_inc(misc_act, 1)
                if ffn:
                    diags(6, 8, 8)
                if ahead:
                    place_max(g + 1, 0)
                if ffn:
                    gexp(7)
                    diags(7, 0, PAIR)
                if att:
                    best_exp(g, 0)
                    if not ahead:
                        best_exp(g, 1)

            schedule(act, setup, build, supertile)

        @block.vector
        def _(dve):
            ts = Tally(SETUP_DVE)
            tb = Tally(BUILD_DVE)
            ta = Tally(ATT_DVE)
            tp = Tally(PREP_DVE)
            tl = Tally(SEL_DVE)

            def setup():
                def step(ins):
                    dve.wait_ge(set_dve, ts(ins.then_inc(set_dve, 1)))

                step(dve.memset(kst[:, :, NTOK:NPAD], 0.0))
                step(dve.memset(kst[SHIFT:P, :, 0:NTOK], 0.0))
                step(dve.memset(kst[SHIFT:SHIFT + 3, :, 0:NTOK], 1.0))
                step(dve.memset(vals_sb[:, :], 0.0))
                step(dve.memset(v4[:, 0:NT - 1, :, E:E + 1], 1.0))
                step(dve.memset(v4[0:NTOK - (NT - 1) * P, NT - 1, :, E:E + 1], 1.0))
                step(dve.memset(h_t[:, NTOK:NPAD], 0.0))
                step(dve.memset(mneg[:, :, :], 0.0))
                step(dve.memset(ones3[:, :], 1.0))
                dve.wait_ge(const_in, 16 * N_CONST)
                step(dve.tensor_copy(idb[:, :], idf[:, :]))
                step(dve.tensor_copy(selw[:, :, :].rearrange("p h r -> p (h r)"), selw_f))
                dve.wait_ge(set_pe, 1)
                step(dve.tensor_tensor(cols[:, 2:3], PV[:, 0:1], cols[:, 3:4], ALU.add))
                dve.wait_ge(set_act, 11)
                step(dve.tensor_copy(brh, brf))
                step(dve.tensor_scalar(brt, brh, masks[:, 0:1], -1.0, ALU.mult, ALU.mult))
                step(dve.tensor_tensor(brt, brt, brf, ALU.add))
                step(dve.tensor_copy(brh, brt))
                step(dve.tensor_scalar(brf, brh, masks[:, 1:2], -1.0, ALU.mult, ALU.mult))
                step(dve.tensor_tensor(brow[:, :], brf, brt, ALU.add))
                ts.end()

            def split(src, parts, w, tally_step):
                tally_step(dve.tensor_copy(parts[:, 0, 0:w], src))
                tally_step(dve.tensor_tensor(src, src, parts[:, 0, 0:w], ALU.subtract))
                tally_step(dve.tensor_copy(parts[:, 1, 0:w], src))
                return dve.tensor_tensor(parts[:, 2, 0:w], src, parts[:, 1, 0:w], ALU.subtract)

            def rsqrt(n, step):
                v, r, t = ln[:, 0, 0:n], ln[:, 3, 0:n], ln[:, 4, 0:n]
                step(dve.tensor_scalar(v, mv[:, 0:n, 1], EPS, None, ALU.add))
                step(dve.tensor_scalar(lnu[:, 0, 0:n], v.bitcast(U32), 1, None, ALU.logical_shift_right))
                step(dve.tensor_scalar(r.bitcast(U32), lnu[:, 0, 0:n], -1.0, RSQRT_SEED, ALU.mult, ALU.add))
                for _ in range(3):
                    step(dve.tensor_tensor(t, v, r, ALU.mult))
                    step(dve.tensor_tensor(t, t, r, ALU.mult))
                    step(dve.tensor_scalar(t, t, -0.5, 1.5, ALU.mult, ALU.add))
                    step(dve.tensor_tensor(r, r, t, ALU.mult))

            def build(b):
                tb.begin(b)

                def step(ins):
                    dve.wait_ge(build_dve, tb(ins.then_inc(build_dve, 1)))

                for c in range(NCH):
                    w, nt = CW[c], CT[c]
                    dve.wait_ge(hrow_ready, b * NCH + c + 1)
                    for t in range(nt):
                        last = dve.bn_stats(st[:, t, :], hrow[:, c % 2, t, :])
                    dve.wait_ge(build_dve, tb(last.then_inc(build_dve, 1)))
                    settled(dve)
                    for t in range(nt):
                        last = dve.bn_aggr(mv[:, t, :], st[:, t, :])
                    dve.wait_ge(build_dve, tb(last.then_inc(build_dve, 1)))
                    rsqrt(nt, step)
                    if c >= 2 or not first(b):
                        dve.wait_ge(xt_ready, b * NCH + c - 1 if c >= 2 else b * NCH)
                    for t in range(nt):
                        last = dve.tensor_scalar(xrow[:, c % 2, t, :], hrow[:, c % 2, t, :], mv[:, t, 0:1],
                                                 ln[:, 3, t:t + 1], ALU.subtract, ALU.mult)
                    last.then_inc(xrow_ready, 1)
                    dve.wait_ge(xrow_ready, b * NCH + c + 1)
                    dve.wait_ge(kf_ready, b * NCH + c + 1)
                    if c or not first(b):
                        dve.wait_ge(place_ready, (b * NCH + c) * H)
                    split(work_f[:, 0:w], parts, w, step).then_inc(kparts_ready, 1)
                    for h in range(0, H, 2):
                        dve.wait_ge(place_ready, (b * NCH + c) * H + h + 1)
                        dve.tensor_copy(kst[0:SROWS, h, c * CH:c * CH + w], MISC[0:SROWS, 0:w]).then_inc(place_dve, 1)
                tb.end()

            def supertile(g, s, att, ffn, taken, ahead):
                ta.begin(g)
                f = g - 1
                f0 = isinstance(f, int) and f == 0

                def step(ins):
                    dve.wait_ge(att_dve, ta(ins.then_inc(att_dve, 1)))

                def pstep(ins):
                    dve.wait_ge(prep_dve, tp(ins.then_inc(prep_dve, 1)))

                def sstep(ins):
                    dve.wait_ge(sel_dve, tl(ins.then_inc(sel_dve, 1)))

                def estep(k, ins):
                    ins.then_inc(exp_dve, 1)
                    dve.wait_ge(exp_dve, f * EXP_DVE + k)

                def dots(j, k0, n):
                    a = j // 4
                    for k in range(k0, k0 + n):
                        if k % 8 == 0:
                            dve.wait_ge(rows_in[2 * (j % RING) + k // 8], f * 256 + (j // RING + 1) * 128)
                        row = gat[:, (j % RING) * PAIR + k, 0:D]
                        dve.tensor_tensor_reduce(row, x2c[:, a, :], row, 1.0, 0.0, ALU.mult, ALU.add,
                                                 xd[:, k:k + 1]).then_inc(exp_dve, 1)

                def gelu_arg(j):
                    k = 2 + j * PAIR_DVE + PAIR
                    dve.wait_ge(exp_dve, f * EXP_DVE + k)
                    if j or not f0:
                        dve.wait_ge(val_ready, f * NPAIR + j)
                    a, c0 = j // 4, (j % 4) * PAIR
                    estep(k + 1, dve.tensor_tensor(gz[:, 0, :], xd[:, :], xd[:, :], ALU.mult))
                    estep(k + 2, dve.tensor_scalar(gz[:, 1, :], gz[:, 0, :], 0.044715, 1.0, ALU.mult, ALU.add))
                    dve.tensor_tensor(gz[:, 2, :], gz[:, 1, :], xd[:, :], ALU.mult).then_inc(z_ready, 1)
                    dve.wait_ge(z_ready, f * NPAIR + j + 1)
                    estep(k + 3, dve.tensor_tensor(gz[:, 3, :], xd[:, :], wn[:, a, c0:c0 + PAIR], ALU.mult))

                def gelu_val(j):
                    k = 2 + j * PAIR_DVE + PAIR + 3
                    dve.wait_ge(e_ready, f * NPAIR + j + 1)
                    estep(k + 1, dve.tensor_scalar(gz[:, 0, :], ge[:, :], 1.0, None, ALU.add))
                    estep(k + 2, dve.reciprocal(gz[:, 1, :], gz[:, 0, :]))
                    if j > 1 or not f0:
                        dve.wait_ge(diag_ready, f * PER_UP + (j - 1) * PAIR)
                    dve.tensor_tensor(gv[:, j % 2, :], gz[:, 1, :], gz[:, 3, :], ALU.mult).then_inc(val_ready, 1)

                def out_add(a):
                    dve.wait_ge(up_done, f * PER_UP + (a + 1) * 64)
                    if not f0:
                        dve.wait_ge(out_stored[a], f * 16)
                    dve.tensor_tensor(ostage[:, a, :], UP[:, 0:D], h1c[:, a, :], ALU.add).then_inc(out_ready, 1)

                def query_parts(n):
                    tp.begin(n)
                    dve.wait_ge(qp_ready, n * 5 + 1)
                    pstep(dve.tensor_scalar(work_f[:, 0:Q], XB[0][:, 0:Q], cols[:, 0:1], None, ALU.add))
                    split(work_f[:, 0:Q], qparts, Q, pstep).then_inc(qparts_ready, 1)

                def reduce(n, h, i, carried=False):
                    a, c = i // NCH, i % NCH
                    dve.wait_ge(r_ready, row_base(n, h, carried) + i + 1)
                    dve.tensor_reduce(mxp[:, a, c:c + 1], RB[i % 2][:, 0:CW[c]], AX_X, ALU.max).then_inc(r_free, 1)

                def minus_max(n, h, step, carried=False):
                    dve.wait_ge(r_free, row_base(n, h, carried) + 2 * NCH)
                    step(dve.tensor_reduce(mx[:, 0, :], mxp[:, :, :], AX_X, ALU.max))
                    if h:
                        dve.wait_ge(misc_ready, n * PER_M + misc_m(h - 1))
                    step(dve.tensor_scalar(mneg[:, :, 0], mx[:, 0, :], -1.0, None, ALU.mult))
                    step(dve.scalar_tensor_tensor(out=mx[:, 1, :], in0=mx[:, 0, :], scalar=-1.0, in1=mneg[:, :, 0],
                                                  op0=ALU.mult, op1=ALU.subtract))
                    step(dve.tensor_copy(mneg[:, :, 1], mx[:, 1, :]))
                    dve.tensor_tensor(mneg[:, :, 2], mx[:, 1, :], mneg[:, :, 1], ALU.subtract).then_inc(mneg_ready, 1)

                def first_max(n, carried):
                    for i in range(2 * NCH):
                        reduce(n, 0, i, carried)
                    minus_max(n, 0, pstep, carried)
                    tp.end()

                def norm_head(h):
                    dve.wait_ge(misc_ready, g * PER_M + misc_o(h))
                    o3 = MISC[:, 0:34].rearrange("p (a c) -> p a c", a=2)
                    step(dve.reciprocal(rcp[:, :, :], o3[:, :, E:E + 1]))
                    dve.tensor_tensor(o_n[:, :, h * E:(h + 1) * E], o3[:, :, 0:E], rcp[:, :, :].to_broadcast([P, 2, E]),
                                      ALU.mult).then_inc(misc_dve, 1)

                def select(n, a, carried, between=None):
                    tl.begin(n * 2 + a)
                    for c4 in range(4):
                        if c4 == 2 and between is not None:
                            between()
                        dve.wait_ge(r_ready, sub_base(n, a, carried) + c4 + 1)
                        settled(dve)
                        for i in range(4):
                            h, c = 2 * c4 + i // 2, i % 2
                            last = dve.max(s8[:, h, c, :], RB[c4 % 2][:, i * NE:(i + 1) * NE])
                        dve.wait_ge(sel_dve, tl(last.then_inc(sel_dve, 1)))
                        settled(dve)
                        for i in range(4):
                            h, c = 2 * c4 + i // 2, i % 2
                            last = dve.max_index(i8[:, h, c, :], s8[:, h, c, :], RB[c4 % 2][:, i * NE:(i + 1) * NE])
                        last.then_inc(r_free, 1)
                    dve.wait_ge(r_free, sub_base(n, a, carried) + 4)
                    sstep(dve.tensor_copy(i8f[:, :, :, :], i8[:, :, :, :]))
                    sstep(dve.tensor_tensor(oneh[:, :, :, :], s8[:, :, 0, :].unsqueeze(3).to_broadcast([P, FH, 8, 8]),
                                           s8[:, :, 1, :].unsqueeze(2).to_broadcast([P, FH, 8, 8]), ALU.add))
                    settled(dve)
                    for h in range(FH):
                        last = dve.max(b8[:, h, :], oneh[:, h, :, :].rearrange("p i j -> p (i j)"))
                    dve.wait_ge(sel_dve, tl(last.then_inc(sel_dve, 1)))
                    settled(dve)
                    for h in range(FH):
                        last = dve.max_index(p8[:, h, :], b8[:, h, :], oneh[:, h, :, :].rearrange("p i j -> p (i j)"))
                    dve.wait_ge(sel_dve, tl(last.then_inc(sel_dve, 1)))
                    dve.tensor_tensor(wsm[:, 0, :, :], b8[:, :, :], b8[:, :, 0:1].to_broadcast([P, FH, 8]),
                                      ALU.subtract).then_inc(best_ready, 1)
                    pos = p8[:, :, :].rearrange("p h k -> p (h k)")
                    sstep(dve.tensor_scalar(pij[:, 0, :], pos, 3, None, ALU.logical_shift_right))
                    sstep(dve.tensor_scalar(pij[:, 1, :], pos, 7, None, ALU.bitwise_and))
                    iota = iot[:, :].unsqueeze(1).to_broadcast([P, FH * 8, 8])
                    o3 = oneh[:, :, :, :].rearrange("p h k i -> p (h k) i")
                    for c in range(2):
                        sstep(dve.tensor_tensor(o3, pij[:, c, :].unsqueeze(2).to_broadcast([P, FH * 8, 8]), iota,
                                               ALU.is_equal))
                        sstep(dve.tensor_tensor(oneh[:, :, :, :], oneh[:, :, :, :],
                                               i8f[:, :, c, :].unsqueeze(2).to_broadcast([P, FH, 8, 8]), ALU.mult))
                        sstep(dve.tensor_reduce(picked[:, c, :], o3, AX_X, ALU.add))
                    dve.wait_ge(bexp_ready, n * 2 + a + 1)
                    sstep(dve.tensor_reduce(wsum[:, :], wsm[:, 1, :, :], AX_X, ALU.add))
                    sstep(dve.reciprocal(wsum[:, :], wsum[:, :]))
                    sstep(dve.tensor_tensor(wn[:, a, :].rearrange("p (h k) -> p h k", h=FH), wsm[:, 1, :, :],
                                           wsum[:, :].unsqueeze(2).to_broadcast([P, FH, 8]), ALU.mult))

                    tl.end()
                    dve.scalar_tensor_tensor(out=idx[a][:, :], in0=picked[:, 0, :], scalar=float(NE),
                                             in1=picked[:, 1, :], op0=ALU.mult, op1=ALU.add).then_inc(idx_ready, 1)

                if att and not taken:
                    query_parts(g)
                    first_max(g, False)
                for h in range(H):
                    behind = taken and h == 0
                    if behind:
                        select(g - 1, 1, True)
                    if ffn and h == 0:
                        if not f0:
                            dve.wait_ge(exp_dve, f * EXP_DVE)
                        dve.wait_ge(x2_ready, g)
                        estep(1, dve.tensor_copy(x2c[:, :, :], x2n[:, :, :]))
                        if not f0:
                            dve.wait_ge(out_ready, f * 2)
                        estep(2, dve.tensor_copy(h1c[:, :, :], h1n[:, :, :]))
                    done = ddone = 0
                    for p in range(XCH):
                        if att and h < H - 1:
                            for i in range(done, done + (R_AT0 if behind else R_AT)[p]):
                                reduce(g, h + 1, i)
                                done += 1
                            if p == 10:
                                minus_max(g, h + 1, step)
                        if att and p == 4 and h:
                            norm_head(h - 1)
                        if ffn:
                            if p == 2 and h >= 2:
                                gelu_val(h - 2)
                            if p == 0 and h == 6:
                                out_add(0)
                            if h >= 1:
                                dots(h - 1, ddone, D_AT[p])
                                ddone += D_AT[p]
                    if ffn and h >= 1:
                        gelu_arg(h - 1)
                if ahead:
                    query_parts(g + 1)
                if att:
                    norm_head(H - 1)
                if ffn:
                    gelu_val(6)
                if att:
                    dve.wait_ge(hres_in, (g + 1) * 16)
                    dve.wait_ge(misc_ready, g * PER_M + 18)
                    dve.tensor_tensor(h1n[:, :, :], MISC[:, 0:Q].rearrange("p (a d) -> p a d", a=2), hres[:, :, :],
                                      ALU.add).then_inc(misc_dve, 1)
                    dve.wait_ge(misc_dve, (g + 1) * PER_MD)
                    for a in range(2):
                        last = dve.bn_stats(st[:, a, :], h1n[:, a, :])
                    last.then_inc(h1_ready, 1)
                    dve.wait_ge(h1_ready, g + 1)
                    settled(dve)
                    for a in range(2):
                        last = dve.bn_aggr(mv[:, a, :], st[:, a, :])
                    dve.wait_ge(att_dve, ta(last.then_inc(att_dve, 1)))
                    rsqrt(2, step)
                    for a in range(2):
                        last = dve.tensor_scalar(x2n[:, a, :], h1n[:, a, :], mv[:, a, 0:1], ln[:, 3, a:a + 1],
                                                 ALU.subtract, ALU.mult)
                    last.then_inc(x2_ready, 1)
                    ta.end()
                if ahead:
                    first_max(g + 1, True)
                if ffn:
                    dots(7, 0, PAIR)
                    gelu_arg(7)
                if att:
                    select(g, 0, ahead, (lambda: gelu_val(7)) if ffn else None)
                elif ffn:
                    gelu_val(7)
                if ffn:
                    out_add(1)
                if att and not ahead:
                    select(g, 1, False)

            schedule(dve, setup, build, supertile)

        @block.tensor
        def _(pe):
            def place_parts(ps, c0, parts, w, h, pattern):
                for j in range(len(pattern) // 2):
                    a, b = pattern[2 * j:2 * j + 2]
                    picks = [(E, a)] if a == b else [(2 * E, a), (0, b)]
                    for i, (at, part) in enumerate(picks):
                        last = pe.matmul(ps[32 * j:32 * j + 32, c0:c0 + w], selw[:, h, at:at + 2 * E], parts[:, part, 0:w],
                                         start=(i == 0), stop=(i == len(picks) - 1))
                return last

            def setup():
                pe.wait_ge(const_in, 16 * N_CONST)
                for n, tap in enumerate(TAP_ORDER):
                    terms = [(pp, s_, o) for pp, s_ in TAPS[tap] for o in range(2)]
                    for i, (pp, s_, o) in enumerate(terms):
                        pe.matmul(XB[n // 4][:, (n % 4) * D:(n % 4 + 1) * D], cw[:, o, s_ * C:(s_ + 1) * C],
                                  lw[:, 2 * pp + o, :], start=(i == 0), stop=(i == len(terms) - 1))
                for k in range(8):
                    last = pe.matmul(PV[:, 0:1], lw[:, k, :], cb[:, k % 2:k % 2 + 1], start=(k == 0), stop=(k == 7))
                last.then_inc(set_pe, 1)
                where = (bank[0], bank[1], UP, MISC)
                for h in range(FH):
                    for c in range(2):
                        r = slice(64 * c, 64 * c + 64)
                        last = pe.matmul(where[2 * c + h // 4][:, (h % 4) * NE:(h % 4 + 1) * NE], fq[r, h, :], fk[r, h, :],
                                         start=True, stop=True)
                last.then_inc(set_pe, 1)
                pe.wait_ge(set_act, 7)
                for h in range(FH):
                    for c in range(2):
                        r = slice(64 * c, 64 * c + 64)
                        last = pe.matmul(where[2 * c + h // 4][0:3, (h % 4) * NE:(h % 4 + 1) * NE], fb[r, h, :], fk[r, h, :],
                                         start=True, stop=True)
                last.then_inc(set_pe, 1)
                pe.wait_ge(set_dve, SETUP_DVE)

            def build(b):
                def tok(n):
                    pe.wait_ge(slab_in[n % 2], dma_count(b, n))
                    if n >= 2:
                        pe.wait_ge(tok_copied, b * (NTOKSTEP + 1) + n - 1)
                    ps = XB[n % 2][:, 0:TSTEP].rearrange("p (i j) -> p i j", j=NP)
                    for k, tap in enumerate(TAP_ORDER):
                        dy, dx = tap
                        i0 = 1 if (n == 0 and dy < 0) else 0
                        i1 = PROWS - 1 if (n == NTOKSTEP - 1 and dy > 1) else PROWS
                        j0, j1 = (1 if dx < 0 else 0), (NP - 1 if dx > 1 else NP)
                        r0, c0 = 2 * i0 + dy + 1, 2 * j0 + dx
                        last = pe.matmul(ps[:, i0:i1, j0:j1], w_tap[:, k, :],
                                         slab[n % 2][:, r0:r0 + 2 * (i1 - i0 - 1) + 1:2, c0:c0 + 2 * (j1 - j0 - 1) + 1:2],
                                         start=(k == 0), stop=(k == len(TAP_ORDER) - 1))
                    last.then_inc(tok_ready, 1)

                if first(b):
                    pe.wait_ge(set_act, 11)
                else:
                    pe.wait_ge(exp_done, b * SUP * PER_X)
                    pe.wait_ge(r_free, b * SUP * PER_R)
                    pe.wait_ge(ot_ready, b * SUP * H)
                    pe.wait_ge(misc_act, b * SUP * PER_MA)
                tok(0)
                tok(1)
                for c in range(NCH):
                    w, nt = CW[c], CT[c]
                    if c == NCH - 1:
                        pe.wait_ge(txt_in, (b + 1) * 16)
                        pe.wait_ge(xt_copied, b * NCH + c)
                        pe.transpose(XB[2][:, 0:P], txt_sb, idf[:, :]).then_inc(txt_ready, 1)
                    pe.wait_ge(tok_copied, b * (NTOKSTEP + 1) + (c + 2 if c < NCH - 1 else NTOKSTEP + 1))
                    if c >= 2:
                        pe.wait_ge(hrow_ready, b * NCH + c - 1)
                    for t in range(nt):
                        last = pe.transpose(RB[c % 2][:, t * P:(t + 1) * P], h_t[:, c * CH + t * P:c * CH + (t + 1) * P], idf[:, :])
                    last.then_inc(lnt_ready, 1)
                    if c + 2 < NTOKSTEP:
                        tok(c + 2)
                    pe.wait_ge(xrow_ready, b * NCH + c + 1)
                    if c:
                        pe.wait_ge(xt_copied, b * NCH + c)
                    for t in range(nt):
                        last = pe.transpose(XB[2][:, t * P:(t + 1) * P], xrow[:, c % 2, t, :], idf[:, :])
                    last.then_inc(xt_ready, 1)
                    pe.wait_ge(xt_copied, b * NCH + c + 1)
                    if c:
                        pe.wait_ge(place_dve, (b * NCH + c) * 4)
                        pe.wait_ge(place_act, (b * NCH + c) * 4)
                    pe.matmul(MISC[:, 0:w], wk_sb[:, :], h_t[:, c * CH:c * CH + w], start=True, stop=True).then_inc(k_ready, 1)
                    for t in range(nt):
                        m = min(P, w - t * P)
                        tok_cols = h_t[:, c * CH + t * P:c * CH + t * P + m]
                        pe.matmul(PV[0:m, t * P:(t + 1) * P], tok_cols, wv_sb[:, :], start=True, stop=False)
                        last = pe.matmul(PV[0:m, t * P:(t + 1) * P], ones3[:, 0:m], brow[:, FH * 2 * NE:FH * 2 * NE + D],
                                         start=False, stop=True)
                    last.then_inc(v_ready, 1)
                    pe.wait_ge(kparts_ready, b * NCH + c + 1)
                    pe.wait_ge(v_copied, b * (NCH + 1) + (c + 1 if c < NCH - 1 else NCH + 1))
                    for h in range(H):
                        if h >= 2:
                            if h % 2 == 0:
                                pe.wait_ge(place_dve, (b * NCH + c) * 4 + h // 2)
                            else:
                                pe.wait_ge(place_act, (b * NCH + c) * 4 + h // 2)
                        last = place_parts(MISC if h % 2 == 0 else PV, 0, parts, w, h, KPART)
                        last.then_inc(place_ready, 1)
                pe.wait_ge(place_dve, (b + 1) * NCH * 4)
                pe.wait_ge(place_act, (b + 1) * NCH * 4)

            def supertile(g, s, att, ffn, taken, ahead):
                f = g - 1

                def ups(j, k0, n):
                    for k in range(k0, k0 + n):
                        u = j * PAIR + k
                        if u % 64 == 0:
                            if u:
                                pe.wait_ge(out_ready, f * 2 + 1)
                            elif not (isinstance(f, int) and f == 0):
                                pe.wait_ge(out_ready, f * 2)
                        pe.wait_ge(diag_ready, f * PER_UP + u + 1)
                        pe.matmul(UP[:, 0:D], diag[:, u % 8, :], gat[:, (j % RING) * PAIR + k, D:2 * D],
                                  start=(u % 64 == 0), stop=(u % 64 == 63)).then_inc(up_done, 1)

                def project(n, s):
                    if not (isinstance(n, int) and n == 0):
                        pe.wait_ge(exp_done, n * PER_X)
                    pe.matmul(XB[0][:, 0:Q], wq_sb[:, :], h_t[:, bass.ds(s * Q, Q)], start=True, stop=True)\
                        .then_inc(qp_ready, 1)

                def place_q(n, u):
                    if u == 0:
                        pe.wait_ge(qparts_ready, n + 1)
                    if u == 3:
                        pe.wait_ge(qp_act, n * 4 + 1)
                    for i in range(2):
                        last = place_parts(XB[(u + 1) % 3], i * Q, qparts, Q, 2 * u + i, QPART)
                    last.then_inc(qp_ready, 1)

                def row_chunk(n, h, i, carried=False):
                    a, c = i // NCH, i % NCH
                    if not (isinstance(n, int) and n == 0 and h == 0 and i < 2):
                        pe.wait_ge(r_free, row_base(n, h, carried) + i - 1)
                    pe.matmul(RB[i % 2][:, 0:CW[c]], qst[0:SROWS, h, a * P:(a + 1) * P], kst[0:SROWS, h, c * CH:c * CH + CW[c]],
                              start=True, stop=True).then_inc(r_ready, 1)

                def sub_chunk(n, a, c4, carried):
                    pe.wait_ge(r_free, sub_base(n, a, carried) + c4 - 1)
                    pe.matmul(RB[c4 % 2][:, :], x2t[:, a * P:(a + 1) * P], w_s[:, c4 * 512:(c4 + 1) * 512], start=True, stop=False)
                    pe.matmul(RB[c4 % 2][:, :], ones3[:, :], brow[:, c4 * 512:(c4 + 1) * 512], start=False, stop=True)\
                        .then_inc(r_ready, 1)

                def turn_max(n, h):
                    pe.wait_ge(mneg_ready, n * H + h + 1)
                    if h == 0:
                        if not (isinstance(n, int) and n == 0):
                            pe.wait_ge(misc_act, n * PER_MA)
                    elif h == 1:
                        pe.wait_ge(misc_act, n * PER_MA + 1)
                    else:
                        pe.wait_ge(misc_dve, n * PER_MD + h - 1)
                    for a in range(2):
                        last = pe.matmul(MISC[SHIFT:P, a * P:(a + 1) * P], mneg[:, a, :], idb[:, :], start=True, stop=True)
                    last.then_inc(misc_ready, 1)

                def turn_out(h):
                    pe.wait_ge(ot_ready, g * H + h + 1)
                    if h < H - 1:
                        pe.wait_ge(misc_act, g * PER_MA + h + 2)
                    else:
                        pe.wait_ge(misc_dve, g * PER_MD + H - 1)
                    for a in range(2):
                        last = pe.matmul(MISC[:, 17 * a:17 * a + 17], o_t[:, a * P:(a + 1) * P], selv[:, :], start=True, stop=True)
                    last.then_inc(misc_ready, 1)

                def weigh(h, p):
                    n = h * XCH + p
                    if p == 0 and not (isinstance(g, int) and g == 0 and h == 0):
                        pe.wait_ge(ot_ready, g * H + h)
                    pe.wait_ge(exp_done, g * PER_X + n + 1)
                    for k in range(2):
                        t = 2 * p + k
                        v0 = (t * H + h) * 17
                        last = pe.matmul(PV[32 * (t % 4):32 * (t % 4) + 32, 0:Q], vals_sb[:, v0:v0 + 32],
                                         probs[:, n % 4, k * Q:(k + 1) * Q], start=(t < 4), stop=(t + 4 >= NT))
                    last.then_inc(pv_done, 1)

                if att and not taken:
                    project(g, s)
                    for u in range(4):
                        place_q(g, u)
                    pe.wait_ge(qp_act, (g + 1) * 4)
                    for i in range(2 * NCH):
                        row_chunk(g, 0, i)
                    turn_max(g, 0)
                for h in range(H):
                    behind = taken and h == 0
                    if att:
                        pe.wait_ge(misc_act, g * PER_MA + h + 1)
                    done, udone, late = 0, 0, PAIR - sum(UP_LATE)
                    for p in range(XCH):
                        if att:
                            n = h * XCH + p
                            if n >= 3:
                                pe.wait_ge(exp_done, g * PER_X + n - 2)
                            elif not (isinstance(g, int) and g == 0):
                                pe.wait_ge(exp_done, g * PER_X)
                            for k in range(2):
                                t = 2 * p + k
                                last = pe.matmul(XB[n % 3][:, k * Q:(k + 1) * Q], kst[:, h, t * P:(t + 1) * P], qst[:, h, :],
                                                 start=True, stop=True)
                            last.then_inc(x_ready, 1)
                            if behind and p < 4:
                                sub_chunk(g - 1, 1, p, True)
                            if h < H - 1:
                                for i in range(done, done + (R_AT0 if behind else R_AT)[p]):
                                    row_chunk(g, h + 1, i)
                                    done += 1
                                if p == 11:
                                    turn_max(g, h + 1)
                            if h and p == 3:
                                turn_out(h - 1)
                            if n >= 2:
                                weigh((n - 2) // XCH, (n - 2) % XCH)
                        if ffn and h >= 3:
                            ups(h - 3, late, UP_LATE[p])
                            late += UP_LATE[p]
                        if ffn and h >= 2:
                            ups(h - 2, udone, UP_AT[p])
                            udone += UP_AT[p]
                if att:
                    weigh(H - 1, XCH - 2)
                    weigh(H - 1, XCH - 1)
                if ffn:
                    ups(5, sum(UP_AT), sum(UP_LATE))
                if ahead:
                    project(g + 1, s + 1)
                if att:
                    turn_out(H - 1)
                if ahead:
                    place_q(g + 1, 0)
                    place_q(g + 1, 1)
                if att:
                    pe.wait_ge(misc_dve, g * PER_MD + H)
                    for a in range(2):
                        last = pe.transpose(MISC[:, a * P:(a + 1) * P], o_n[:, a, :], idf[:, :])
                    last.then_inc(misc_ready, 1)
                    pe.wait_ge(misc_act, g * PER_MA + H + 1)
                    for a in range(2):
                        pe.matmul(MISC[:, a * P:(a + 1) * P], c_t[:, a * P:(a + 1) * P], wo_sb[:, :], start=True, stop=False)
                        last = pe.matmul(MISC[:, a * P:(a + 1) * P], ones3[:, :], brow[:, FH * 2 * NE + D:], start=False, stop=True)
                    last.then_inc(misc_ready, 1)
                if ahead:
                    place_q(g + 1, 2)
                    place_q(g + 1, 3)
                if ffn:
                    ups(6, 0, 8)
                if ahead:
                    pe.wait_ge(qp_act, (g + 2) * 4)
                    row_chunk(g + 1, 0, 0, True)
                    row_chunk(g + 1, 0, 1, True)
                if att:
                    pe.wait_ge(x2_ready, g + 1)
                    for a in range(2):
                        last = pe.transpose(MISC[:, a * P:(a + 1) * P], x2n[:, a, :], idf[:, :])
                    last.then_inc(misc_ready, 1)
                if not ahead and ffn:
                    ups(6, 8, 8)
                if ahead:
                    for i in range(2, 2 * NCH):
                        row_chunk(g + 1, 0, i, True)
                        if ffn and i < 10:
                            ups(6, 6 + i, 1)
                if att:
                    pe.wait_ge(misc_act, (g + 1) * PER_MA)
                    for c4 in range(4):
                        sub_chunk(g, 0, c4, ahead)
                        if c4 == 1 and ahead:
                            turn_max(g + 1, 0)
                if ffn:
                    ups(7, 0, PAIR)
                if att and not ahead:
                    for c4 in range(4):
                        sub_chunk(g, 1, c4, False)

            schedule(pe, setup, build, supertile)


def kernel(x, txt, L0_tok_conv_w, L0_tok_conv_b, L0_tok_lin_w, L0_tok_lin_b, L0_attn_Wq, L0_attn_Wk, L0_attn_Wv,
           L0_attn_bq, L0_attn_bk, L0_attn_bv, L0_attn_Wo, L0_attn_bo, L0_ffn_Wq, L0_ffn_bq, L0_ffn_keys,
           L0_ffn_w_down_embed, L0_ffn_w_up_embed):
    import numpy as np
    import concourse.bacc as bacc
    from concourse.bass_utils import run_bass_kernel_spmd

    def by_head(w):
        return np.transpose(np.asarray(w), (1, 0, 2)).reshape(D, D)

    sel_w = np.zeros((H, E, H, 4, E), np.float32)
    for h in range(H):
        for e in range(E):
            sel_w[h, e, h, 1:3, e] = 1

    sel_v = np.zeros((P, 17), np.float32)
    for group in range(4):
        sel_v[32 * group + np.arange(17), np.arange(17)] = 1
    bv, bo = np.asarray(L0_attn_bv).reshape(D), np.asarray(L0_attn_bo)
    arrays = {
        "x": x, "txt": txt, "conv_w": L0_tok_conv_w, "conv_b": np.asarray(L0_tok_conv_b).reshape(2, P).T,
        "lin_wt": np.asarray(L0_tok_lin_w).T, "lin_b": np.asarray(L0_tok_lin_b).reshape(D, 1),
        "wq": by_head(L0_attn_Wq), "wk": by_head(L0_attn_Wk), "wv": by_head(L0_attn_Wv),
        "bq": np.asarray(L0_attn_bq).reshape(D, 1), "bk": np.asarray(L0_attn_bk).reshape(D, 1),
        "bvo": np.stack([np.concatenate([bv, bo])] * 3), "wo": L0_attn_Wo,
        "ffn_wq": L0_ffn_Wq, "ffn_bq": np.stack([np.asarray(L0_ffn_bq)] * 3, axis=1),
        "ffn_keys_t": np.transpose(np.asarray(L0_ffn_keys), (1, 3, 0, 2)),
        "table": np.concatenate([np.asarray(L0_ffn_w_down_embed), np.asarray(L0_ffn_w_up_embed)], axis=1),
        "ident": np.eye(P, dtype=np.float32), "sel_w": sel_w.reshape(P, -1), "sel_v": sel_v,
        "part_masks": np.array([[0, 0], [1, 0], [1, 1]], np.float32),
        "iota8": np.stack([np.arange(8, dtype=np.float32)] * P),
    }
    nc = bacc.Bacc("TRN2", target_bir_lowering=False, num_devices=1)
    in_map, args = {}, []
    for name, a in arrays.items():
        a = np.ascontiguousarray(a)
        in_map[f"in_{name}"] = a
        args.append(nc.dram_tensor(f"in_{name}", a.shape, mybir.dt.from_np(a.dtype), kind="ExternalInput").ap())
    args.append(nc.dram_tensor("out_rows", (B * NPAD, D), F32, kind="ExternalOutput").ap())
    early_fusion(nc, *args)
    r = run_bass_kernel_spmd(nc, [in_map], core_ids=[0])
    return r.results[0]["out_rows"].reshape(B, NPAD, D)[:, :NTOK, :]
```

```python
from contextlib import ExitStack

import concourse.bass as bass
from concourse import mybir

F32 = mybir.dt.float32
BF16 = mybir.dt.bfloat16
U32 = mybir.dt.uint32
ACT = mybir.ActivationFunctionType
ALU = mybir.AluOpType
AX_X = mybir.AxisListType.X

P = 128
B, C, IMG = 4, 128, 112
D = 128
H, E = 8, 16
NP = IMG // 2
NTXT = 128
NTOK = NP * NP + NTXT
NT = -(-NTOK // P)
NPAD = NT * P
Q = 256
SUP = NPAD // Q
G_ALL = B * SUP
FH, TOPK, NE = 8, 8, 128
EPS = 1e-5

KPART = (0, 0, 1, 1, 0, 2)
QPART = (0, 1, 0, 1, 2, 0)
SROWS = len(KPART) * E
SHIFT = SROWS

SHIFTS = ((0, 0), (0, -1), (0, 1), (-1, 0), (1, 0))
TAPS = {}
for _py in range(2):
    for _px in range(2):
        for _s, (_dy, _dx) in enumerate(SHIFTS):
            TAPS.setdefault((_py + _dy, _px + _dx), []).append((_py * 2 + _px, _s))
TAP_ORDER = sorted(TAPS, key=lambda t: (t[0] not in (0, 1)) or (t[1] not in (0, 1)))

PROWS = 8
NTOKSTEP = NP // PROWS
TSTEP = PROWS * NP
CH = 512
NCH = -(-NTOK // CH)
CW = [min(CH, NTOK - c * CH) for c in range(NCH)]
CT = [-(-w // P) for w in CW]
XCH = NT // 2

PER_R = H * 2 * NCH + 2 * 4
PER_X = H * XCH
PAIR = 16
NPAIR = 2 * FH * TOPK // PAIR
PER_UP = NPAIR * PAIR
RING = 4
R_LEAD = (2, 1, 1, 2, 1, 1, 2, 1, 0, 0, 0, 0, 0)
R_EARLY = (0, 0, 0, 0, 0, 0, 0, 0, 0, 0, 1, 1, 1)
D_AT = (0, 0, 1, 0, 1, 2, 0, 2, 2, 2, 0, 3, 3)
DIAG_AT = (0, 0, 0, 2, 2, 1, 2, 1, 2, 1, 2, 1, 2)
UP_AT = (0, 0, 0, 0, 0, 2, 1, 2, 1, 2, 2, 1, 1)
UP_LATE = (2, 2, 0, 0, 0, 0, 0, 0, 0, 0, 0, 0, 0)
MAX_AT = 8
SUB_HEADS = ((1, 2), (5, 6))
SUB_AT = {(SUB_HEADS[a][c4 // 2], 8 + c4 % 2): (a, c4) for a in range(2) for c4 in range(4)}
SUMS_AT = {(2, 11): 0, (6, 11): 1}
TOP_AT = {(3, 3): 0, (7, 3): 1}
BEST_AT = {(3, 6): 0, (7, 6): 1}
PICK_AT = {(3, 5): (0, 0), (3, 8): (0, 1), (7, 5): (1, 0), (7, 8): (1, 1)}
ROWS_AT = {(3, 10): 0, (7, 10): 1}
DOTS_LAG, UPS_LAG = 5, 6
assert sum(R_LEAD) + sum(R_EARLY) == 2 * NCH and sum(D_AT) == sum(DIAG_AT) == sum(UP_AT) + sum(UP_LATE) == PAIR
GELU_C = 2.0 * 0.7978845608028654
RSQRT_SEED = float(0x5F3759DF)
GELU_DVE = 5
SETUP_DVE = 18
BUILD_DVE = 140
ATT_DVE = 21
NORM_DVE = 17
PREP_DVE = 6
SEL_DVE = 10
PICK_DVE = 9


def zero(n):
    return isinstance(n, int) and n == 0


def row_base(g, h):
    if zero(g):
        return h * 2 * NCH
    return g * PER_R - 8 + h * 2 * NCH + 2 * sum(h > at + 1 for heads in SUB_HEADS for at in heads)


def sub_index(g, a, c4, att):
    if not att:
        return g * PER_R - 8 + 4 * a + c4
    return row_base(g, SUB_HEADS[a][c4 // 2] + 1) + 2 * NCH + c4 % 2


def row_chunks(g, h, p, ahead):
    chunks = []
    for later, at, start in ((1, R_LEAD, sum(R_EARLY)), (2, R_EARLY, 0)):
        n, head = (g, h + later) if h + later < H else (g + 1, h + later - H)
        if h + later < H or ahead:
            chunks += [(n, head, start + sum(at[:p]) + i) for i in range(at[p])]
    return chunks


def dots_of(h, f):
    return (h - DOTS_LAG, f) if h >= DOTS_LAG else (h - DOTS_LAG + NPAIR, f - 1)


def ups_of(h, f):
    return (h - UPS_LAG, f) if h >= UPS_LAG else (h - UPS_LAG + NPAIR, f - 1)


def dma_count(b, n, per=(NTOKSTEP + 1) // 2, other=NTOKSTEP // 2):
    return 16 * (b * (per if n % 2 == 0 else other) + n // 2 + 1)


class Tally:

    def __init__(self, per):
        self.per, self.base, self.k = per, 0, 0

    def begin(self, index):
        self.base, self.k = index * self.per, 0

    def __call__(self, instruction):
        self.k += 1
        return self.base + self.k

    def end(self):
        assert self.k == self.per, (self.k, self.per)


def early_fusion(nc, x, txt, conv_w, conv_b, lin_wt, lin_b, wq, wk, wv, bq, bk, bvo, wo,
                 ffn_wq, ffn_bq, ffn_keys_t, table, ident, sel_w, sel_v, part_masks, iota8, out):
    with ExitStack() as ctx:
        def sb(name, shape, dt):
            return ctx.enter_context(nc.sbuf_tensor(name, shape, dt))

        def sem(name):
            return ctx.enter_context(nc.semaphore(name))

        kst = sb("key_stack", [P, H, NPAD], BF16)
        vals_sb = sb("values", [P, NT * H * 17 + 15], F32)
        v4 = vals_sb[:, 0:NT * H * 17].rearrange("p (t h c) -> p t h c", t=NT, c=17)
        h_t = sb("h_t", [P, NPAD], F32)
        gat = sb("gathered", [P, RING * PAIR, 2 * D], F32)
        qst = sb("query_stack", [P, H, Q], BF16)
        xrow = (qst[:, :, :].rearrange("p h q -> p (h q)").bitcast(F32)
                .rearrange("p (c t d) -> p c t d", c=2, t=4))
        probs = sb("probs", [P, 4, 2 * Q], F32)
        diag = sb("diag", [P, 8, D], F32)
        hrow = diag[:, :, :].rearrange("p (c t) d -> p c t d", c=2)
        slab = [sb(f"slab{i}", [P, 2 * PROWS + 2, IMG], F32) for i in range(1)]
        slab.append(probs[:, :, :].rearrange("p a b -> p (a b)")[:, 0:(2 * PROWS + 2) * IMG]
                    .rearrange("p (r w) -> p r w", w=IMG))
        w_tap = sb("w_tap", [P, 12, D], F32)
        w_s = sb("w_s", [P, FH * 2 * NE], F32)
        wq_sb = sb("wq_sb", [P, D], F32)
        wk_sb = sb("wk_sb", [P, D], F32)
        wv_sb = sb("wv_sb", [P, D], F32)
        wo_sb = sb("wo_sb", [P, D], F32)
        cols = sb("cols", [P, 4], F32)
        brow = sb("brow", [3, FH * 2 * NE + 2 * D], BF16)
        idf = sb("idf", [P, P], F32)
        idb = sb("idb", [P, P], BF16)
        selw = sb("selw", [P, H, 4 * E], BF16)
        selv = sb("selv", [P, 17], F32)
        masks = sb("masks", [3, 2], F32)
        iot = sb("iot", [P, 8], F32)
        ones3 = sb("ones3", [3, P], BF16)
        qparts = sb("qparts", [P, 3, Q], BF16)
        shared = sb("shared", [P, 3 * CH // 2], F32)
        parts = shared[:, :].bitcast(BF16).rearrange("p (a n) -> p a n", a=3)
        o_n = shared[:, 0:2 * D].rearrange("p (a d) -> p a d", a=2)
        c_t = shared[:, 2 * D:2 * D + Q]
        s8 = shared[:, 512:640].rearrange("p (h c k) -> p h c k", h=FH, c=2)
        i8 = shared[:, 640:768].bitcast(U32).rearrange("p (h c k) -> p h c k", h=FH, c=2)
        st = sb("st", [P, 4, 6], F32)
        mv = sb("mv", [P, 4, 2], F32)
        ln = sb("ln", [P, 6, 4], F32)
        lnu = sb("lnu", [P, 2, 4], U32)
        hres = sb("hres", [P, 2, D], F32)
        mxp = sb("mxp", [P, 2, NCH], F32)
        mx = sb("mx", [P, 2, 2], F32)
        mneg = sb("mneg", [P, 2, 32], BF16)
        o_t = sb("o_t", [P, Q], F32)
        rcp = sb("rcp", [P, 2, 1], F32)
        h1n = sb("h1n", [P, 2, D], F32)
        h1c = sb("h1c", [P, 2, D], F32)
        x2n = sb("x2n", [P, 2, D], F32)
        x2c = sb("x2c", [P, 2, D], F32)
        x2t = c_t
        i8f = sb("i8f", [P, FH, 2, 8], F32)
        b8 = sb("b8", [P, FH, 8], F32)
        p8 = sb("p8", [P, FH, 8], U32)
        pij = sb("pij", [P, 2, FH * 8], U32)
        oneh = sb("oneh", [P, FH, 8, 8], F32)
        work_f = oneh[:, :, :, :].rearrange("p h k i -> p (h k i)")
        picked = sb("picked", [P, 2, FH * 8], F32)
        wsm = sb("wsm", [P, 2, FH, 8], F32)
        wsum = sb("wsum", [P, FH], F32)
        wn = sb("wn", [P, 2, FH * 8], F32)
        idx = [sb(f"idx{a}", [P, FH * 8], U32) for a in range(2)]
        xd = sb("xd", [P, 2, PAIR], F32)
        gz = sb("gz", [P, 4, PAIR], F32)
        ge = sb("ge", [P, PAIR], F32)
        gv = sb("gv", [P, 2, PAIR], F32)
        ostage = sb("ostage", [P, 2, D], F32)
        txt_sb = o_t[:, 0:D]

        gflat = gat[:, :, :].rearrange("p a b -> p (a b)")
        cw = gflat[:, 0:1280].rearrange("p (o n) -> p o n", o=2)
        lw = gflat[:, 1280:2304].rearrange("p (k d) -> p k d", k=8)
        fq = gflat[:, 2304:3328].rearrange("p (h d) -> p h d", h=FH)
        fk = gflat[:, 3328:4352].rearrange("p (h e) -> p h e", h=FH)
        fb = gflat[:, 4352:4376].rearrange("p (h r) -> p h r", h=FH)
        cb = gflat[:, 4376:4378]
        NB = FH * 2 * NE + 2 * D
        brf = gflat[0:3, 4400:4400 + NB]
        brt = gflat[0:3, 6800:6800 + NB]
        selw_f = gflat[:, 9200:9200 + H * 4 * E]
        brh = gflat[0:3, 14000:14000 + NB // 2].bitcast(BF16)

        bank = [ctx.enter_context(nc.psum_tensor(f"bank{i}", [P, 512], F32)) for i in range(8)]
        RB, XB, PV, UP, MISC = bank[0:2], bank[2:5], bank[5], bank[6], bank[7]

        h_dram = nc.dram_tensor("h_rows", [B * NPAD, D], F32, kind="Internal").ap()

        const_in = sem("const_in")
        table_in = sem("table_in")
        set_pe = sem("set_pe")
        set_act = sem("set_act")
        set_dve = sem("set_dve")
        slab_in = [sem("slab_in0"), sem("slab_in1")]
        txt_in = sem("txt_in")
        txt_ready = sem("txt_ready")
        tok_ready = sem("tok_ready")
        tok_copied = sem("tok_copied")
        lnt_ready = sem("lnt_ready")
        hrow_ready = sem("hrow_ready")
        hrow_stored = [sem("hrow_stored0"), sem("hrow_stored1")]
        xrow_ready = sem("xrow_ready")
        xt_ready = sem("xt_ready")
        xt_copied = sem("xt_copied")
        k_ready = sem("k_ready")
        kf_ready = sem("kf_ready")
        kparts_ready = sem("kparts_ready")
        v_ready = sem("v_ready")
        v_copied = sem("v_copied")
        place_ready = sem("place_ready")
        place_dve = sem("place_dve")
        place_act = sem("place_act")
        build_dve = sem("build_dve")
        hres_in = sem("hres_in")
        qp_ready = sem("qp_ready")
        qparts_ready = sem("qparts_ready")
        qp_act = sem("qp_act")
        r_ready = sem("r_ready")
        r_free = sem("r_free")
        mneg_ready = sem("mneg_ready")
        max_turned = sem("max_turned")
        max_placed = sem("max_placed")
        x_ready = sem("x_ready")
        exp_done = sem("exp_done")
        pv_done = sem("pv_done")
        ot_ready = sem("ot_ready")
        out_turned = sem("out_turned")
        out_normed = sem("out_normed")
        heads_turned = sem("heads_turned")
        heads_copied = sem("heads_copied")
        projected = sem("projected")
        h1_summed = sem("h1_summed")
        h1_ready = sem("h1_ready")
        x2_ready = sem("x2_ready")
        x2_turned = sem("x2_turned")
        x2t_ready = sem("x2t_ready")
        best_ready = sem("best_ready")
        bexp_ready = sem("bexp_ready")
        att_dve = sem("att_dve")
        norm_dve = sem("norm_dve")
        prep_dve = sem("prep_dve")
        sel_dve = sem("sel_dve")
        pick_dve = sem("pick_dve")
        idx_ready = sem("idx_ready")
        rows_in = [sem(f"rows_in{i}") for i in range(2 * RING)]
        z_ready = sem("z_ready")
        e_ready = sem("e_ready")
        val_ready = sem("val_ready")
        diag_ready = sem("diag_ready")
        up_done = sem("up_done")
        out_ready = sem("out_ready")
        out_stored = [sem("out_stored0"), sem("out_stored1")]
        dots_done = sem("dots_done")
        gelu_dve = sem("gelu_dve")
        x2c_ready = sem("x2c_ready")
        residual_kept = sem("residual_kept")

        N_CONST = 19

        def schedule(eng, setup, build, supertile):
            setup()
            build(0)
            supertile(0, 0, True, False, False, False, True)
            supertile(1, 1, True, True, False, True, True)
            supertile(2, 2, True, True, True, True, True)
            with eng.Fori(3, SUP - 1) as s:
                supertile(s, s, True, True, True, True, True)
            supertile(SUP - 1, SUP - 1, True, True, True, True, False)
            with eng.Fori(1, B) as b:
                build(b)
                supertile(b * SUP, 0, True, True, True, False, True)
                with eng.Fori(1, SUP - 1) as s:
                    supertile(b * SUP + s, s, True, True, True, True, True)
                supertile(b * SUP + SUP - 1, SUP - 1, True, True, True, True, False)
            supertile(G_ALL, None, False, True, True, False, False)
            supertile(G_ALL + 1, None, False, False, True, False, False)

        passed = {nc.vector: sem("passed_dve"), nc.gpsimd: sem("passed_pool"), nc.sync: sem("passed_sp")}

        def settled(eng):
            eng.sem_inc(passed[eng], 1)

        block = ctx.enter_context(nc.Block())

        @block.sync
        def _(sp):
            def setup():
                pairs = [
                    (cw, conv_w.rearrange("(o p) n -> p o n", p=P)),
                    (lw, lin_wt.rearrange("(k p) d -> p k d", p=P)),
                    (cb, conv_b),
                    (fq, ffn_wq.rearrange("(h p) d -> p h d", p=P)),
                    (fk, ffn_keys_t.rearrange("c f h e -> (c f) h e")),
                    (fb, ffn_bq.rearrange("(h p) r -> p h r", p=P)),
                    (wq_sb[:, :], wq), (wk_sb[:, :], wk), (wv_sb[:, :], wv), (wo_sb[:, :], wo),
                    (cols[:, 0:1], bq), (cols[:, 1:2], bk), (cols[:, 3:4], lin_b),
                    (brf[:, FH * 2 * NE:], bvo),
                    (idf[:, :], ident),
                    (selw_f, sel_w), (selv[:, :], sel_v),
                    (masks[:, :], part_masks), (iot[:, :], iota8),
                ]
                assert len(pairs) == N_CONST, len(pairs)
                for dst, src in pairs:
                    sp.dma_start(dst, src).then_inc(const_in, 16)

            def build(b):
                def load_slab(n):
                    i = n % 2
                    if n >= 2:
                        sp.wait_ge(tok_ready, b * NTOKSTEP + n - 1)
                    elif not zero(b):
                        sp.wait_ge(tok_ready, b * NTOKSTEP)
                        sp.wait_ge(pv_done, b * SUP * PER_X)
                    lo, hi = max(0, 2 * PROWS * n - 1), min(IMG, 2 * PROWS * (n + 1) + 1)
                    at = 1 if n == 0 else 0
                    sp.dma_start(slab[i][:, at:at + hi - lo, :],
                                 x[bass.ds(b, 1), :, lo:hi, :].rearrange("b c r w -> (b c) r w")).then_inc(slab_in[i], 16)

                load_slab(0)
                load_slab(1)
                if not zero(b):
                    sp.wait_ge(out_turned, b * SUP * H)
                sp.dma_start(txt_sb, txt[bass.ds(b, 1), :, :].rearrange("b t d -> (b t) d")).then_inc(txt_in, 16)
                for c in range(NCH):
                    if c + 2 < NTOKSTEP:
                        load_slab(c + 2)
                    sp.wait_ge(hrow_ready, b * NCH + c + 1)
                    rows = h_dram[bass.ds(b * NPAD + c * CH, CT[c] * P), :]
                    sp.dma_start(rows.rearrange("(t p) d -> p t d", p=P), hrow[:, c % 2, 0:CT[c], :])\
                        .then_inc(hrow_stored[c % 2], 16)
                sp.wait_ge(hrow_stored[0], dma_count(b, NCH - 1))
                sp.wait_ge(hrow_stored[1], dma_count(b, NCH - 2))
                settled(sp)

            def supertile(g, s, att, sel, left, taken, ahead):
                if att:
                    if not zero(g):
                        sp.wait_ge(h1_ready, g)
                    sp.dma_start(hres[:, :, :], h_dram[bass.ds(g * Q, Q), :].rearrange("(t p) d -> p t d", p=P))\
                        .then_inc(hres_in, 16)
                if left:
                    for a in range(2):
                        sp.wait_ge(out_ready, (g - 2) * 2 + a + 1)
                        sp.dma_start(out[bass.ds((g - 2) * Q + a * P, P), :], ostage[:, a, :]).then_inc(out_stored[a], 16)

            schedule(sp, setup, build, supertile)
            for o in out_stored:
                sp.wait_ge(o, 16 * G_ALL)

        @block.gpsimd
        def _(pool):
            def gather(f, first_f):
                for j in range(NPAIR):
                    a = j // 4
                    if j % 4 == 0:
                        pool.wait_ge(idx_ready, f * 2 + a + 1)
                    if not (first_f and j < RING):
                        pool.wait_ge(up_done, f * PER_UP + (j - RING + 1) * PAIR)
                    settled(pool)
                    for k in range(PAIR):
                        col = (j % 4) * PAIR + k
                        pool.indirect_dma_start(
                            gat[:, (j % RING) * PAIR + k, :], None, table,
                            bass.IndirectOffsetOnAxis(ap=idx[a][:, col:col + 1], axis=0),
                        ).then_inc(rows_in[2 * (j % RING) + k // 8], 16)

            gather(0, True)
            with pool.Fori(1, G_ALL) as f:
                gather(f, False)

        @block.scalar
        def _(act):
            def setup():
                act.wait_ge(set_pe, 1)
                for i in range(3):
                    act.activation(w_tap[:, 4 * i:4 * i + 4, :], XB[i][:, :].rearrange("p (t d) -> p t d", d=D),
                                   ACT.Copy).then_inc(set_act, 1)
                act.wait_ge(set_pe, 2)
                ws4 = w_s[:, :].rearrange("p (h c e) -> p h c e", h=FH, c=2)
                for i, bk_ in enumerate((bank[0], bank[1], UP, MISC)):
                    c, hh = i // 2, i % 2
                    act.activation(ws4[:, 4 * hh:4 * hh + 4, c, :], bk_[:, :].rearrange("p (h e) -> p h e", e=NE),
                                   ACT.Copy).then_inc(set_act, 1)
                act.wait_ge(set_pe, 3)
                bs4 = brf[:, 0:FH * 2 * NE].rearrange("p (h c e) -> p h c e", h=FH, c=2)
                for i, bk_ in enumerate((bank[0], bank[1], UP, MISC)):
                    c, hh = i // 2, i % 2
                    act.activation(bs4[:, 4 * hh:4 * hh + 4, c, :], bk_[0:3, :].rearrange("p (h e) -> p h e", e=NE),
                                   ACT.Copy).then_inc(set_act, 1)

            def build(b):
                def tok(n):
                    act.wait_ge(tok_ready, b * NTOKSTEP + n + 1)
                    act.activation(h_t[:, n * TSTEP:(n + 1) * TSTEP], XB[n % 2][:, 0:TSTEP], ACT.Identity,
                                   bias=cols[:, 2:3]).then_inc(tok_copied, 1)

                def place(c):
                    for h in range(1, H, 2):
                        act.wait_ge(place_ready, (b * NCH + c) * H + h + 1)
                        act.activation(kst[0:SROWS, h, c * CH:c * CH + CW[c]], PV[0:SROWS, 0:CW[c]], ACT.Copy)\
                            .then_inc(place_act, 1)

                if zero(b):
                    act.wait_ge(set_dve, SETUP_DVE)
                tok(0)
                tok(1)
                for c in range(NCH):
                    w, nt = CW[c], CT[c]
                    if c == NCH - 1:
                        act.wait_ge(txt_ready, b + 1)
                        act.activation(h_t[:, NP * NP:NTOK], XB[2][:, 0:P], ACT.Copy).then_inc(tok_copied, 1)
                    act.wait_ge(lnt_ready, b * NCH + c + 1)
                    if c >= 2:
                        act.wait_ge(hrow_stored[c % 2], dma_count(b, c - 2))
                        act.wait_ge(xrow_ready, b * NCH + c - 1)
                    elif not zero(b):
                        act.wait_ge(hrow_stored[c % 2], dma_count(b, c) - 16)
                    act.activation(hrow[:, c % 2, 0:nt, :], RB[c % 2][:, 0:nt * P].rearrange("p (t d) -> p t d", d=D),
                                   ACT.Copy).then_inc(hrow_ready, 1)
                    if c:
                        place(c - 1)
                    if c + 2 < NTOKSTEP:
                        tok(c + 2)
                    act.wait_ge(xt_ready, b * NCH + c + 1)
                    act.activation(h_t[:, c * CH:c * CH + nt * P], XB[2][:, 0:nt * P], ACT.Copy).then_inc(xt_copied, 1)
                    act.wait_ge(k_ready, b * NCH + c + 1)
                    if c or not zero(b):
                        act.wait_ge(kparts_ready, b * NCH + c)
                    act.activation(work_f[:, 0:w], MISC[:, 0:w], ACT.Identity, bias=cols[:, 1:2]).then_inc(kf_ready, 1)
                    act.wait_ge(v_ready, b * NCH + c + 1)
                    full = w // P
                    last = act.activation(v4[:, 4 * c:4 * c + full, :, 0:E],
                                          PV[:, 0:full * P].rearrange("p (t h e) -> p t h e", t=full, e=E), ACT.Copy)
                    if w % P:
                        r = w % P
                        last.then_inc(v_copied, 1)
                        last = act.activation(v4[0:r, 4 * c + full, :, 0:E],
                                              PV[0:r, full * P:(full + 1) * P].rearrange("p (h e) -> p h e", e=E), ACT.Copy)
                    last.then_inc(v_copied, 1)
                place(NCH - 1)
                act.wait_ge(hrow_stored[0], dma_count(b, NCH - 1))
                act.wait_ge(hrow_stored[1], dma_count(b, NCH - 2))

            def supertile(g, s, att, sel, left, taken, ahead):
                def gexp(j, f):
                    act.wait_ge(z_ready, f * NPAIR + j + 1)
                    act.activation(ge[:, :], gz[:, 2, :], ACT.Exp, scale=-GELU_C).then_inc(e_ready, 1)

                def diags(j, f, i0, n):
                    for k in range(i0, i0 + n):
                        if k == 0:
                            act.wait_ge(val_ready, f * NPAIR + j + 1)
                        u = j * PAIR + k
                        if not (zero(f) and u < 8):
                            act.wait_ge(up_done, f * PER_UP + u - 7)
                        act.activation(diag[:, u % 8, :], idf[:, :], ACT.Copy, scale=gv[:, j % 2, k:k + 1])\
                            .then_inc(diag_ready, 1)

                def place_q(n, u):
                    act.wait_ge(qp_ready, n * 5 + 2 + u)
                    act.activation(qst[0:SROWS, 2 * u:2 * u + 2, :],
                                   MISC[0:SROWS, :].rearrange("p (h q) -> p h q", q=Q), ACT.Copy).then_inc(qp_act, 1)

                def place_max(n, h):
                    act.wait_ge(max_turned, n * H + h + 1)
                    act.activation(qst[SHIFT:P, h, :], MISC[SHIFT:P, 0:Q], ACT.Copy).then_inc(max_placed, 1)

                def head_out(n, h):
                    act.wait_ge(pv_done, n * PER_X + (h + 1) * XCH)
                    if not (zero(n) and h == 0):
                        act.wait_ge(out_turned, n * H + h)
                    act.activation(o_t[:, :], PV[:, 0:Q], ACT.Copy).then_inc(ot_ready, 1)

                def heads_copy(n):
                    act.wait_ge(heads_turned, n + 1)
                    act.activation(c_t, MISC[:, 0:Q], ACT.Copy).then_inc(heads_copied, 1)

                if att and not taken:
                    for u in range(4):
                        place_q(g, u)
                    place_max(g, 0)
                for h in range(H):
                    j, f = ups_of(h, g - 1)
                    busy = sel if h >= UPS_LAG else left
                    done = 0
                    for p in range(XCH):
                        if att:
                            n = h * XCH + p
                            act.wait_ge(x_ready, g * PER_X + n + 1)
                            if not (zero(g) and n < 4):
                                act.wait_ge(pv_done, g * PER_X + n - 3)
                            act.activation(probs[:, n % 4, :], XB[n % 3][:, :], ACT.Exp, scale=E ** -0.5)\
                                .then_inc(exp_done, 1)
                            if p == 1:
                                if h:
                                    head_out(g, h - 1)
                                elif taken:
                                    head_out(g - 1, H - 1)
                            if taken and h == 0:
                                if p == 2:
                                    place_q(g, 3)
                                if p == 6:
                                    heads_copy(g - 1)
                            if ahead and h in (2, 4, 6) and p == 7:
                                place_q(g + 1, h // 2 - 1)
                            if p == MAX_AT + 2:
                                if h < H - 1:
                                    place_max(g, h + 1)
                                elif ahead:
                                    place_max(g + 1, 0)
                        if sel and h == 1 and p == 3:
                            act.wait_ge(x2_turned, g)
                            act.activation(x2t, MISC[:, 0:Q], ACT.Copy).then_inc(x2t_ready, 1)
                        if sel and (h, p) in BEST_AT:
                            act.wait_ge(best_ready, (g - 1) * 2 + BEST_AT[h, p] + 1)
                            act.activation(wsm[:, 1, :, :], wsm[:, 0, :, :], ACT.Exp).then_inc(bexp_ready, 1)
                        if busy:
                            if p == 1:
                                gexp(j, f)
                            diags(j, f, done, DIAG_AT[p])
                            done += DIAG_AT[p]
                if att and not ahead:
                    head_out(g, H - 1)
                    heads_copy(g)

            schedule(act, setup, build, supertile)

        @block.vector
        def _(dve):
            ts = Tally(SETUP_DVE)
            tb = Tally(BUILD_DVE)
            ta = Tally(ATT_DVE)
            tp = Tally(PREP_DVE)
            tn = Tally(NORM_DVE)
            tl = Tally(SEL_DVE)
            tk = Tally(PICK_DVE)

            def setup():
                def step(ins):
                    dve.wait_ge(set_dve, ts(ins.then_inc(set_dve, 1)))

                step(dve.memset(kst[:, :, NTOK:NPAD], 0.0))
                step(dve.memset(kst[SHIFT:P, :, 0:NTOK], 0.0))
                step(dve.memset(kst[SHIFT:SHIFT + 3, :, 0:NTOK], 1.0))
                step(dve.memset(vals_sb[:, :], 0.0))
                step(dve.memset(v4[:, 0:NT - 1, :, E:E + 1], 1.0))
                step(dve.memset(v4[0:NTOK - (NT - 1) * P, NT - 1, :, E:E + 1], 1.0))
                step(dve.memset(h_t[:, NTOK:NPAD], 0.0))
                step(dve.memset(mneg[:, :, :], 0.0))
                step(dve.memset(ones3[:, :], 1.0))
                dve.wait_ge(const_in, 16 * N_CONST)
                step(dve.tensor_copy(idb[:, :], idf[:, :]))
                step(dve.tensor_copy(selw[:, :, :].rearrange("p h r -> p (h r)"), selw_f))
                dve.wait_ge(set_pe, 1)
                step(dve.tensor_tensor(cols[:, 2:3], PV[:, 0:1], cols[:, 3:4], ALU.add))
                dve.wait_ge(set_act, 11)
                step(dve.tensor_copy(brh, brf))
                step(dve.tensor_scalar(brt, brh, masks[:, 0:1], -1.0, ALU.mult, ALU.mult))
                step(dve.tensor_tensor(brt, brt, brf, ALU.add))
                step(dve.tensor_copy(brh, brt))
                step(dve.tensor_scalar(brf, brh, masks[:, 1:2], -1.0, ALU.mult, ALU.mult))
                step(dve.tensor_tensor(brow[:, :], brf, brt, ALU.add))
                ts.end()

            def split(src, parts, w, tally_step):
                tally_step(dve.tensor_copy(parts[:, 0, 0:w], src))
                tally_step(dve.tensor_tensor(src, src, parts[:, 0, 0:w], ALU.subtract))
                tally_step(dve.tensor_copy(parts[:, 1, 0:w], src))
                return dve.tensor_tensor(parts[:, 2, 0:w], src, parts[:, 1, 0:w], ALU.subtract)

            def rsqrt(n, step):
                v, r, t = ln[:, 0, 0:n], ln[:, 3, 0:n], ln[:, 4, 0:n]
                step(dve.tensor_scalar(v, mv[:, 0:n, 1], EPS, None, ALU.add))
                step(dve.tensor_scalar(lnu[:, 0, 0:n], v.bitcast(U32), 1, None, ALU.logical_shift_right))
                step(dve.tensor_scalar(r.bitcast(U32), lnu[:, 0, 0:n], -1.0, RSQRT_SEED, ALU.mult, ALU.add))
                for _ in range(3):
                    step(dve.tensor_tensor(t, v, r, ALU.mult))
                    step(dve.tensor_tensor(t, t, r, ALU.mult))
                    step(dve.tensor_scalar(t, t, -0.5, 1.5, ALU.mult, ALU.add))
                    step(dve.tensor_tensor(r, r, t, ALU.mult))

            def build(b):
                tb.begin(b)

                def step(ins):
                    dve.wait_ge(build_dve, tb(ins.then_inc(build_dve, 1)))

                def place(c, h):
                    if c >= 0:
                        dve.wait_ge(place_ready, (b * NCH + c) * H + h + 1)
                        dve.tensor_copy(kst[0:SROWS, h, c * CH:c * CH + CW[c]], MISC[0:SROWS, 0:CW[c]]).then_inc(place_dve, 1)

                for c in range(NCH):
                    w, nt = CW[c], CT[c]
                    place(c - 1, 0)
                    dve.wait_ge(hrow_ready, b * NCH + c + 1)
                    for t in range(nt):
                        last = dve.bn_stats(st[:, t, :], hrow[:, c % 2, t, :])
                    dve.wait_ge(build_dve, tb(last.then_inc(build_dve, 1)))
                    settled(dve)
                    for t in range(nt):
                        last = dve.bn_aggr(mv[:, t, :], st[:, t, :])
                    dve.wait_ge(build_dve, tb(last.then_inc(build_dve, 1)))
                    place(c - 1, 2)
                    rsqrt(nt, step)
                    place(c - 1, 4)
                    if c >= 2 or not zero(b):
                        dve.wait_ge(xt_ready, b * NCH + c - 1 if c >= 2 else b * NCH)
                    for t in range(nt):
                        last = dve.tensor_scalar(xrow[:, c % 2, t, :], hrow[:, c % 2, t, :], mv[:, t, 0:1],
                                                 ln[:, 3, t:t + 1], ALU.subtract, ALU.mult)
                    last.then_inc(xrow_ready, 1)
                    dve.wait_ge(xrow_ready, b * NCH + c + 1)
                    place(c - 1, 6)
                    dve.wait_ge(kf_ready, b * NCH + c + 1)
                    if c or not zero(b):
                        dve.wait_ge(place_ready, (b * NCH + c) * H)
                    split(work_f[:, 0:w], parts, w, step).then_inc(kparts_ready, 1)
                for h in range(0, H, 2):
                    place(NCH - 1, h)
                tb.end()

            def supertile(g, s, att, sel, left, taken, ahead):
                if att:
                    ta.begin(g)

                def step(ins):
                    ins.then_inc(att_dve, 1)
                    fill()
                    dve.wait_ge(att_dve, ta(ins))

                def pstep(ins):
                    ins.then_inc(prep_dve, 1)
                    fill()
                    dve.wait_ge(prep_dve, tp(ins))

                def nstep(ins):
                    ins.then_inc(norm_dve, 1)
                    fill()
                    dve.wait_ge(norm_dve, tn(ins))

                def sstep(ins):
                    ins.then_inc(sel_dve, 1)
                    fill()
                    dve.wait_ge(sel_dve, tl(ins))

                def dot(j, f, k):
                    if k % 8 == 0:
                        dve.wait_ge(rows_in[2 * (j % RING) + k // 8], f * 256 + (j // RING + 1) * 128)
                    row = gat[:, (j % RING) * PAIR + k, 0:D]
                    dve.tensor_tensor_reduce(row, x2c[:, j // 4, :], row, 1.0, 0.0, ALU.mult, ALU.add,
                                             xd[:, j % 2, k:k + 1]).then_inc(dots_done, 1)

                def kstep(ins):
                    ins.then_inc(pick_dve, 1)
                    fill()
                    dve.wait_ge(pick_dve, tk(ins))

                dotting = [None, None, PAIR]

                def fill():
                    j, f, k = dotting
                    if k < PAIR:
                        dot(j, f, k)
                        dotting[2] = k + 1

                def gelu_step(f, k, ins):
                    ins.then_inc(gelu_dve, 1)
                    fill()
                    dve.wait_ge(gelu_dve, f * NPAIR * GELU_DVE + k)

                def gelu_arg(j, f):
                    k = j * GELU_DVE
                    x = xd[:, j % 2, :]
                    dve.wait_ge(dots_done, f * PER_UP + (j + 1) * PAIR)
                    if j or not zero(f):
                        dve.wait_ge(val_ready, f * NPAIR + j)
                    a, c0 = j // 4, (j % 4) * PAIR
                    gelu_step(f, k + 1, dve.tensor_tensor(gz[:, 0, :], x, x, ALU.mult))
                    gelu_step(f, k + 2, dve.tensor_scalar(gz[:, 1, :], gz[:, 0, :], 0.044715, 1.0, ALU.mult, ALU.add))
                    dve.tensor_tensor(gz[:, 2, :], gz[:, 1, :], x, ALU.mult).then_inc(z_ready, 1)
                    gelu_step(f, k + 3, dve.tensor_tensor(gz[:, 3, :], x, wn[:, a, c0:c0 + PAIR], ALU.mult))

                def gelu_val(j, f):
                    k = j * GELU_DVE + 3
                    dve.wait_ge(e_ready, f * NPAIR + j + 1)
                    gelu_step(f, k + 1, dve.tensor_scalar(gz[:, 0, :], ge[:, :], 1.0, None, ALU.add))
                    gelu_step(f, k + 2, dve.reciprocal(gz[:, 1, :], gz[:, 0, :]))
                    if j > 1 or not zero(f):
                        dve.wait_ge(diag_ready, f * PER_UP + (j - 1) * PAIR)
                    dve.tensor_tensor(gv[:, j % 2, :], gz[:, 1, :], gz[:, 3, :], ALU.mult).then_inc(val_ready, 1)

                def out_add(a, f):
                    dve.wait_ge(up_done, f * PER_UP + (a + 1) * 64)
                    if not zero(f):
                        dve.wait_ge(out_stored[a], f * 16)
                    dve.wait_ge(residual_kept, f + 1)
                    dve.tensor_tensor(ostage[:, a, :], UP[:, 0:D], h1c[:, a, :], ALU.add).then_inc(out_ready, 1)

                def query_parts(n):
                    tp.begin(n)
                    dve.wait_ge(qp_ready, n * 5 + 1)
                    pstep(dve.tensor_scalar(work_f[:, 0:Q], MISC[:, 0:Q], cols[:, 0:1], None, ALU.add))
                    split(work_f[:, 0:Q], qparts, Q, pstep).then_inc(qparts_ready, 1)

                def reduce(n, h, i):
                    a, c = i // NCH, i % NCH
                    dve.wait_ge(r_ready, row_base(n, h) + i + 1)
                    dve.tensor_reduce(mxp[:, a, c:c + 1], RB[i % 2][:, 0:CW[c]], AX_X, ALU.max).then_inc(r_free, 1)

                def minus_max(n, h, step):
                    dve.wait_ge(r_free, row_base(n, h) + 2 * NCH)
                    step(dve.tensor_reduce(mx[:, 0, :], mxp[:, :, :], AX_X, ALU.max))
                    if not (zero(n) and h == 0):
                        dve.wait_ge(max_turned, n * H + h)
                    step(dve.tensor_scalar(mneg[:, :, 0], mx[:, 0, :], -1.0, None, ALU.mult))
                    dve.scalar_tensor_tensor(out=mneg[:, :, 1], in0=mx[:, 0, :], scalar=-1.0, in1=mneg[:, :, 0],
                                             op0=ALU.mult, op1=ALU.subtract).then_inc(mneg_ready, 1)

                def norm_head(n, h, step):
                    dve.wait_ge(out_turned, n * H + h + 1)
                    o3 = MISC[:, 0:34].rearrange("p (a c) -> p a c", a=2)
                    step(dve.reciprocal(rcp[:, :, :], o3[:, :, E:E + 1]))
                    dve.tensor_tensor(o_n[:, :, h * E:(h + 1) * E], o3[:, :, 0:E], rcp[:, :, :].to_broadcast([P, 2, E]),
                                      ALU.mult).then_inc(out_normed, 1)

                def last_head(n):
                    tn.begin(n)
                    norm_head(n, H - 1, nstep)

                def layer_norm(n):
                    dve.wait_ge(hres_in, (n + 1) * 16)
                    dve.wait_ge(projected, n + 1)
                    dve.tensor_tensor(h1n[:, :, :], MISC[:, 0:Q].rearrange("p (a d) -> p a d", a=2), hres[:, :, :],
                                      ALU.add).then_inc(h1_summed, 1)
                    dve.wait_ge(h1_summed, n + 1)
                    for a in range(2):
                        last = dve.bn_stats(st[:, a, :], h1n[:, a, :])
                    last.then_inc(h1_ready, 1)
                    dve.wait_ge(h1_ready, n + 1)
                    settled(dve)
                    for a in range(2):
                        last = dve.bn_aggr(mv[:, a, :], st[:, a, :])
                    nstep(last)
                    rsqrt(2, nstep)
                    if not zero(n):
                        dve.wait_ge(x2_turned, n)
                    for a in range(2):
                        last = dve.tensor_scalar(x2n[:, a, :], h1n[:, a, :], mv[:, a, 0:1], ln[:, 3, a:a + 1],
                                                 ALU.subtract, ALU.mult)
                    last.then_inc(x2_ready, 1)
                    tn.end()

                def sub_top(n, a, c4):
                    if c4 == 0:
                        tl.begin(n * 2 + a)
                    dve.wait_ge(r_ready, sub_index(n + 1, a, c4, att) + 1)
                    settled(dve)
                    for i in range(4):
                        h, c = 2 * c4 + i // 2, i % 2
                        last = dve.max(s8[:, h, c, :], RB[c4 % 2][:, i * NE:(i + 1) * NE])
                    sstep(last)
                    settled(dve)
                    for i in range(4):
                        h, c = 2 * c4 + i // 2, i % 2
                        last = dve.max_index(i8[:, h, c, :], s8[:, h, c, :], RB[c4 % 2][:, i * NE:(i + 1) * NE])
                    last.then_inc(r_free, 1)
                    if c4 == 3:
                        dve.wait_ge(r_free, sub_index(n + 1, a, 3, att) + 1)

                def pair_sums():
                    sstep(dve.tensor_copy(i8f[:, :, :, :], i8[:, :, :, :]))
                    sstep(dve.tensor_tensor(oneh[:, :, :, :], s8[:, :, 0, :].unsqueeze(3).to_broadcast([P, FH, 8, 8]),
                                            s8[:, :, 1, :].unsqueeze(2).to_broadcast([P, FH, 8, 8]), ALU.add))
                    settled(dve)
                    for h in range(FH):
                        last = dve.max(b8[:, h, :], oneh[:, h, :, :].rearrange("p i j -> p (i j)"))
                    sstep(last)

                def pair_top(n, a):
                    settled(dve)
                    for h in range(FH):
                        last = dve.max_index(p8[:, h, :], b8[:, h, :], oneh[:, h, :, :].rearrange("p i j -> p (i j)"))
                    sstep(last)
                    dve.tensor_tensor(wsm[:, 0, :, :], b8[:, :, :], b8[:, :, 0:1].to_broadcast([P, FH, 8]),
                                      ALU.subtract).then_inc(best_ready, 1)
                    pos = p8[:, :, :].rearrange("p h k -> p (h k)")
                    sstep(dve.tensor_scalar(pij[:, 0, :], pos, 3, None, ALU.logical_shift_right))
                    sstep(dve.tensor_scalar(pij[:, 1, :], pos, 7, None, ALU.bitwise_and))
                    tl.end()

                def pick(n, a, c):
                    if c == 0:
                        tk.begin(n * 2 + a)
                    iota = iot[:, :].unsqueeze(1).to_broadcast([P, FH * 8, 8])
                    o3 = oneh[:, :, :, :].rearrange("p h k i -> p (h k) i")
                    kstep(dve.tensor_tensor(o3, pij[:, c, :].unsqueeze(2).to_broadcast([P, FH * 8, 8]), iota,
                                            ALU.is_equal))
                    kstep(dve.tensor_tensor(oneh[:, :, :, :], oneh[:, :, :, :],
                                            i8f[:, :, c, :].unsqueeze(2).to_broadcast([P, FH, 8, 8]), ALU.mult))
                    kstep(dve.tensor_reduce(picked[:, c, :], o3, AX_X, ALU.add))

                def table_rows(n, a):
                    dve.scalar_tensor_tensor(out=idx[a][:, :], in0=picked[:, 0, :], scalar=float(NE),
                                             in1=picked[:, 1, :], op0=ALU.mult, op1=ALU.add).then_inc(idx_ready, 1)
                    dve.wait_ge(bexp_ready, n * 2 + a + 1)
                    kstep(dve.tensor_reduce(wsum[:, :], wsm[:, 1, :, :], AX_X, ALU.add))
                    kstep(dve.reciprocal(wsum[:, :], wsum[:, :]))
                    kstep(dve.tensor_tensor(wn[:, a, :].rearrange("p (h k) -> p h k", h=FH), wsm[:, 1, :, :],
                                            wsum[:, :].unsqueeze(2).to_broadcast([P, FH, 8]), ALU.mult))
                    tk.end()

                if att and not taken:
                    query_parts(g)
                    for i in range(2 * NCH):
                        reduce(g, 0, i)
                    minus_max(g, 0, pstep)
                    tp.end()
                    for i in range(sum(R_EARLY)):
                        reduce(g, 1, i)
                for h in range(H):
                    dj, df = dots_of(h, g - 1)
                    vj, vf = ups_of(h, g - 1)
                    valuing = sel if h >= UPS_LAG else left
                    if sel and h == DOTS_LAG:
                        if left:
                            dve.wait_ge(dots_done, (g - 1) * PER_UP)
                        dve.wait_ge(x2_ready, g)
                        dve.tensor_copy(x2c[:, :, :], x2n[:, :, :]).then_inc(x2c_ready, 1)
                        dve.wait_ge(x2c_ready, g)
                    if sel if h >= DOTS_LAG else left:
                        dotting[:] = [dj, df, 0]
                    for p in range(XCH):
                        if att:
                            if p == MAX_AT and h < H - 1:
                                minus_max(g, h + 1, step)
                            elif p == MAX_AT and ahead:
                                minus_max(g + 1, 0, pstep)
                                tp.end()
                            for chunk in row_chunks(g, h, p, ahead):
                                reduce(*chunk)
                            if p == 5 and h:
                                norm_head(g, h - 1, step)
                            if taken and h == 0 and p == 4:
                                last_head(g - 1)
                            if taken and h == 0 and p == 9:
                                layer_norm(g - 1)
                            if ahead and h == 1 and p == 7:
                                query_parts(g + 1)
                        if sel and (h, p) in SUB_AT:
                            sub_top(g - 1, *SUB_AT[h, p])
                        if sel and (h, p) in SUMS_AT:
                            pair_sums()
                        if sel and (h, p) in TOP_AT:
                            pair_top(g - 1, TOP_AT[h, p])
                        if sel and (h, p) in PICK_AT:
                            pick(g - 1, *PICK_AT[h, p])
                        if sel and (h, p) in ROWS_AT:
                            table_rows(g - 1, ROWS_AT[h, p])
                        if valuing and p == 0:
                            gelu_arg(vj, vf)
                        if valuing and p == 2:
                            gelu_val(vj, vf)
                        if left and h == 2 and p == 3:
                            out_add(0, g - 2)
                        if h == 6 and p == 3:
                            if left:
                                out_add(1, g - 2)
                                dve.wait_ge(out_ready, (g - 1) * 2)
                            if sel:
                                dve.tensor_copy(h1c[:, :, :], h1n[:, :, :]).then_inc(residual_kept, 1)
                        while dotting[2] < min(PAIR, sum(D_AT[:p + 1])):
                            fill()
                if att:
                    if not ahead:
                        last_head(g)
                        layer_norm(g)
                    ta.end()
                settled(dve)

            schedule(dve, setup, build, supertile)

        @block.tensor
        def _(pe):
            def place_parts(ps, c0, parts, w, h, pattern):
                for j in range(len(pattern) // 2):
                    a, b = pattern[2 * j:2 * j + 2]
                    picks = [(E, a)] if a == b else [(2 * E, a), (0, b)]
                    for i, (at, part) in enumerate(picks):
                        last = pe.matmul(ps[32 * j:32 * j + 32, c0:c0 + w], selw[:, h, at:at + 2 * E], parts[:, part, 0:w],
                                         start=(i == 0), stop=(i == len(picks) - 1))
                return last

            def setup():
                pe.wait_ge(const_in, 16 * N_CONST)
                for n, tap in enumerate(TAP_ORDER):
                    terms = [(pp, s_, o) for pp, s_ in TAPS[tap] for o in range(2)]
                    for i, (pp, s_, o) in enumerate(terms):
                        pe.matmul(XB[n // 4][:, (n % 4) * D:(n % 4 + 1) * D], cw[:, o, s_ * C:(s_ + 1) * C],
                                  lw[:, 2 * pp + o, :], start=(i == 0), stop=(i == len(terms) - 1))
                for k in range(8):
                    last = pe.matmul(PV[:, 0:1], lw[:, k, :], cb[:, k % 2:k % 2 + 1], start=(k == 0), stop=(k == 7))
                last.then_inc(set_pe, 1)
                where = (bank[0], bank[1], UP, MISC)
                for h in range(FH):
                    for c in range(2):
                        r = slice(64 * c, 64 * c + 64)
                        last = pe.matmul(where[2 * c + h // 4][:, (h % 4) * NE:(h % 4 + 1) * NE], fq[r, h, :], fk[r, h, :],
                                         start=True, stop=True)
                last.then_inc(set_pe, 1)
                pe.wait_ge(set_act, 7)
                for h in range(FH):
                    for c in range(2):
                        r = slice(64 * c, 64 * c + 64)
                        last = pe.matmul(where[2 * c + h // 4][0:3, (h % 4) * NE:(h % 4 + 1) * NE], fb[r, h, :], fk[r, h, :],
                                         start=True, stop=True)
                last.then_inc(set_pe, 1)
                pe.wait_ge(set_dve, SETUP_DVE)

            def build(b):
                def tok(n, k0=0, k1=len(TAP_ORDER)):
                    if n >= NTOKSTEP:
                        return
                    if k0 == 0:
                        pe.wait_ge(slab_in[n % 2], dma_count(b, n))
                        if n >= 2:
                            pe.wait_ge(tok_copied, b * (NTOKSTEP + 1) + n - 1)
                    ps = XB[n % 2][:, 0:TSTEP].rearrange("p (i j) -> p i j", j=NP)
                    for k in range(k0, k1):
                        tap = TAP_ORDER[k]
                        dy, dx = tap
                        i0 = 1 if (n == 0 and dy < 0) else 0
                        i1 = PROWS - 1 if (n == NTOKSTEP - 1 and dy > 1) else PROWS
                        j0, j1 = (1 if dx < 0 else 0), (NP - 1 if dx > 1 else NP)
                        r0, c0 = 2 * i0 + dy + 1, 2 * j0 + dx
                        last = pe.matmul(ps[:, i0:i1, j0:j1], w_tap[:, k, :],
                                         slab[n % 2][:, r0:r0 + 2 * (i1 - i0 - 1) + 1:2, c0:c0 + 2 * (j1 - j0 - 1) + 1:2],
                                         start=(k == 0), stop=(k == len(TAP_ORDER) - 1))
                    if k1 == len(TAP_ORDER):
                        last.then_inc(tok_ready, 1)

                def place(c, h):
                    if h == 0:
                        pe.wait_ge(kparts_ready, b * NCH + c + 1)
                        pe.wait_ge(v_copied, b * (NCH + 1) + (c + 1 if c < NCH - 1 else NCH + 1))
                    elif h >= 2:
                        pe.wait_ge(place_dve if h % 2 == 0 else place_act, (b * NCH + c) * 4 + h // 2)
                    last = place_parts(MISC if h % 2 == 0 else PV, 0, parts, CW[c], h, KPART)
                    last.then_inc(place_ready, 1)

                if zero(b):
                    pe.wait_ge(set_act, 11)
                else:
                    pe.wait_ge(exp_done, b * SUP * PER_X)
                    pe.wait_ge(r_free, b * SUP * PER_R - 8)
                    pe.wait_ge(ot_ready, b * SUP * H)
                    pe.wait_ge(h1_summed, b * SUP)
                tok(0)
                tok(1)
                for c in range(NCH):
                    w, nt = CW[c], CT[c]
                    if c == NCH - 1:
                        pe.wait_ge(txt_in, (b + 1) * 16)
                        pe.wait_ge(xt_copied, b * NCH + c)
                        pe.transpose(XB[2][:, 0:P], txt_sb, idf[:, :]).then_inc(txt_ready, 1)
                    pe.wait_ge(tok_copied, b * (NTOKSTEP + 1) + (c + 2 if c < NCH - 1 else NTOKSTEP + 1))
                    if c >= 2:
                        pe.wait_ge(hrow_ready, b * NCH + c - 1)
                    for t in range(nt):
                        last = pe.transpose(RB[c % 2][:, t * P:(t + 1) * P], h_t[:, c * CH + t * P:c * CH + (t + 1) * P], idf[:, :])
                    last.then_inc(lnt_ready, 1)
                    if c == 0:
                        tok(2)
                    else:
                        tok(c + 2, 0, 2)
                        for h in range(H):
                            place(c - 1, h)
                            tok(c + 2, *((2 * h + 2, 2 * h + 4) if h < 2 else (h + 4, h + 5)))
                    pe.wait_ge(xrow_ready, b * NCH + c + 1)
                    if c:
                        pe.wait_ge(xt_copied, b * NCH + c)
                    for t in range(nt):
                        last = pe.transpose(XB[2][:, t * P:(t + 1) * P], xrow[:, c % 2, t, :], idf[:, :])
                    last.then_inc(xt_ready, 1)
                    pe.wait_ge(xt_copied, b * NCH + c + 1)
                    if c:
                        pe.wait_ge(place_dve, (b * NCH + c) * 4)
                        pe.wait_ge(place_act, (b * NCH + c) * 4)
                    pe.matmul(MISC[:, 0:w], wk_sb[:, :], h_t[:, c * CH:c * CH + w], start=True, stop=True).then_inc(k_ready, 1)
                    for t in range(nt):
                        m = min(P, w - t * P)
                        tok_cols = h_t[:, c * CH + t * P:c * CH + t * P + m]
                        pe.matmul(PV[0:m, t * P:(t + 1) * P], tok_cols, wv_sb[:, :], start=True, stop=False)
                        last = pe.matmul(PV[0:m, t * P:(t + 1) * P], ones3[:, 0:m], brow[:, FH * 2 * NE:FH * 2 * NE + D],
                                         start=False, stop=True)
                    last.then_inc(v_ready, 1)
                for h in range(H):
                    place(NCH - 1, h)
                pe.wait_ge(place_dve, (b + 1) * NCH * 4)
                pe.wait_ge(place_act, (b + 1) * NCH * 4)

            def supertile(g, s, att, sel, left, taken, ahead):
                def ups(j, f, k0, n):
                    for k in range(k0, k0 + n):
                        u = j * PAIR + k
                        if u % 64 == 0:
                            if u:
                                pe.wait_ge(out_ready, f * 2 + 1)
                            elif not zero(f):
                                pe.wait_ge(out_ready, f * 2)
                        pe.wait_ge(diag_ready, f * PER_UP + u + 1)
                        pe.matmul(UP[:, 0:D], diag[:, u % 8, :], gat[:, (j % RING) * PAIR + k, D:2 * D],
                                  start=(u % 64 == 0), stop=(u % 64 == 63)).then_inc(up_done, 1)

                def project(n, s):
                    pe.matmul(MISC[:, 0:Q], wq_sb[:, :], h_t[:, bass.ds(s * Q, Q)], start=True, stop=True)\
                        .then_inc(qp_ready, 1)

                def place_q(n, u):
                    for i in range(2):
                        last = place_parts(MISC, i * Q, qparts, Q, 2 * u + i, QPART)
                    last.then_inc(qp_ready, 1)

                def row_chunk(n, h, i):
                    a, c = i // NCH, i % NCH
                    if not (zero(n) and h == 0 and i < 2):
                        pe.wait_ge(r_free, row_base(n, h) + i - 1)
                    pe.matmul(RB[i % 2][:, 0:CW[c]], qst[0:SROWS, h, a * P:(a + 1) * P], kst[0:SROWS, h, c * CH:c * CH + CW[c]],
                              start=True, stop=True).then_inc(r_ready, 1)

                def sub_chunk(a, c4):
                    pe.wait_ge(r_free, sub_index(g, a, c4, att) - 1)
                    pe.wait_ge(x2t_ready, g)
                    pe.matmul(RB[c4 % 2][:, :], x2t[:, a * P:(a + 1) * P], w_s[:, c4 * 512:(c4 + 1) * 512], start=True, stop=False)
                    pe.matmul(RB[c4 % 2][:, :], ones3[:, :], brow[:, c4 * 512:(c4 + 1) * 512], start=False, stop=True)\
                        .then_inc(r_ready, 1)

                def turn_max(n, h):
                    pe.wait_ge(mneg_ready, n * H + h + 1)
                    for a in range(2):
                        last = pe.matmul(MISC[SHIFT:P, a * P:(a + 1) * P], mneg[:, a, :], idb[:, :], start=True, stop=True)
                    last.then_inc(max_turned, 1)

                def turn_out(n, h):
                    pe.wait_ge(ot_ready, n * H + h + 1)
                    for a in range(2):
                        last = pe.matmul(MISC[:, 17 * a:17 * a + 17], o_t[:, a * P:(a + 1) * P], selv[:, :], start=True, stop=True)
                    last.then_inc(out_turned, 1)

                def turn_heads(n):
                    pe.wait_ge(out_normed, (n + 1) * H)
                    for a in range(2):
                        last = pe.transpose(MISC[:, a * P:(a + 1) * P], o_n[:, a, :], idf[:, :])
                    last.then_inc(heads_turned, 1)

                def project_out(n):
                    pe.wait_ge(heads_copied, n + 1)
                    for a in range(2):
                        pe.matmul(MISC[:, a * P:(a + 1) * P], c_t[:, a * P:(a + 1) * P], wo_sb[:, :], start=True, stop=False)
                        last = pe.matmul(MISC[:, a * P:(a + 1) * P], ones3[:, :], brow[:, FH * 2 * NE + D:], start=False, stop=True)
                    last.then_inc(projected, 1)

                def weigh(m, h, p):
                    n = h * XCH + p
                    if p == 0 and not (zero(m) and h == 0):
                        pe.wait_ge(ot_ready, m * H + h)
                    pe.wait_ge(exp_done, m * PER_X + n + 1)
                    for k in range(2):
                        t = 2 * p + k
                        v0 = (t * H + h) * 17
                        last = pe.matmul(PV[32 * (t % 4):32 * (t % 4) + 32, 0:Q], vals_sb[:, v0:v0 + 32],
                                         probs[:, n % 4, k * Q:(k + 1) * Q], start=(t < 4), stop=(t + 4 >= NT))
                    last.then_inc(pv_done, 1)

                if att and not taken:
                    project(g, s)
                    pe.wait_ge(qparts_ready, g + 1)
                    for u in range(4):
                        place_q(g, u)
                        pe.wait_ge(qp_act, g * 4 + u + 1)
                    for i in range(2 * NCH):
                        row_chunk(g, 0, i)
                    turn_max(g, 0)
                    for i in range(sum(R_EARLY)):
                        row_chunk(g, 1, i)
                for h in range(H):
                    if att:
                        pe.wait_ge(max_placed, g * H + h + 1)
                    if att and ahead and h == H - 1:
                        pe.wait_ge(qp_act, (g + 1) * 4 + 3)
                    j, f = ups_of(h, g - 1)
                    jt, ft = ups_of(h - 1, g - 1) if h else ups_of(H - 1, g - 2)
                    busy = sel if h >= UPS_LAG else left
                    trail = sel if h > UPS_LAG else left and (h > 0 or taken)
                    udone, late = 0, PAIR - sum(UP_LATE)
                    for p in range(XCH):
                        if att:
                            n = h * XCH + p
                            if n >= 3:
                                pe.wait_ge(exp_done, g * PER_X + n - 2)
                            elif not zero(g):
                                pe.wait_ge(exp_done, g * PER_X - (1 if n == 0 else 0))
                            for k in range(2):
                                t = 2 * p + k
                                last = pe.matmul(XB[n % 3][:, k * Q:(k + 1) * Q], kst[:, h, t * P:(t + 1) * P], qst[:, h, :],
                                                 start=True, stop=True)
                            last.then_inc(x_ready, 1)
                            for chunk in row_chunks(g, h, p, ahead):
                                row_chunk(*chunk)
                            if h < H - 1 or ahead:
                                nn, nh = (g, h + 1) if h < H - 1 else (g + 1, 0)
                                if p == MAX_AT + 2:
                                    if ahead and h in (2, 4, 6):
                                        pe.wait_ge(qp_act, (g + 1) * 4 + h // 2)
                                    elif ahead and h == 1:
                                        pe.wait_ge(qparts_ready, g + 2)
                                    elif h:
                                        pe.wait_ge(out_normed, g * H + h)
                                    elif taken:
                                        pe.wait_ge(h1_summed, g)
                                    turn_max(nn, nh)
                            if h == 0 and taken:
                                if p == 1:
                                    place_q(g, 3)
                                if p == 3:
                                    pe.wait_ge(qp_act, g * 4 + 4)
                                    turn_out(g - 1, H - 1)
                                if p == 6:
                                    turn_heads(g - 1)
                                if p == 7:
                                    project_out(g - 1)
                            if h and p == 4:
                                if h == 1 and sel:
                                    pe.wait_ge(x2t_ready, g)
                                turn_out(g, h - 1)
                            if ahead and h in (1, 2, 4, 6) and p == 6:
                                pe.wait_ge(out_normed, g * H + h)
                                if h == 1:
                                    project(g + 1, s + 1)
                                else:
                                    if h == 2:
                                        pe.wait_ge(qparts_ready, g + 2)
                                    place_q(g + 1, h // 2 - 1)
                            if n >= 2:
                                weigh(g, (n - 2) // XCH, (n - 2) % XCH)
                            elif taken:
                                weigh(g - 1, H - 1, XCH - 2 + n)
                        if sel and h == 1 and p == 2:
                            pe.wait_ge(x2_ready, g)
                            for a in range(2):
                                last = pe.transpose(MISC[:, a * P:(a + 1) * P], x2n[:, a, :], idf[:, :])
                            last.then_inc(x2_turned, 1)
                        if sel and (h, p + 1) in SUB_AT:
                            sub_chunk(*SUB_AT[h, p + 1])
                        if trail:
                            ups(jt, ft, late, UP_LATE[p])
                            late += UP_LATE[p]
                        if busy:
                            ups(j, f, udone, UP_AT[p])
                            udone += UP_AT[p]
                if att and not ahead:
                    weigh(g, H - 1, XCH - 2)
                    weigh(g, H - 1, XCH - 1)
                if sel and not ahead:
                    ups(*ups_of(H - 1, g - 1), sum(UP_AT), sum(UP_LATE))
                if att and not ahead:
                    pe.wait_ge(out_normed, g * H + H - 1)
                    turn_out(g, H - 1)
                    turn_heads(g)
                    project_out(g)

            schedule(pe, setup, build, supertile)


def kernel(x, txt, L0_tok_conv_w, L0_tok_conv_b, L0_tok_lin_w, L0_tok_lin_b, L0_attn_Wq, L0_attn_Wk, L0_attn_Wv,
           L0_attn_bq, L0_attn_bk, L0_attn_bv, L0_attn_Wo, L0_attn_bo, L0_ffn_Wq, L0_ffn_bq, L0_ffn_keys,
           L0_ffn_w_down_embed, L0_ffn_w_up_embed):
    import numpy as np
    import concourse.bacc as bacc
    from concourse.bass_utils import run_bass_kernel_spmd

    def by_head(w):
        return np.transpose(np.asarray(w), (1, 0, 2)).reshape(D, D)

    sel_w = np.zeros((H, E, H, 4, E), np.float32)
    for h in range(H):
        for e in range(E):
            sel_w[h, e, h, 1:3, e] = 1

    sel_v = np.zeros((P, 17), np.float32)
    for group in range(4):
        sel_v[32 * group + np.arange(17), np.arange(17)] = 1
    bv, bo = np.asarray(L0_attn_bv).reshape(D), np.asarray(L0_attn_bo)
    arrays = {
        "x": x, "txt": txt, "conv_w": L0_tok_conv_w, "conv_b": np.asarray(L0_tok_conv_b).reshape(2, P).T,
        "lin_wt": np.asarray(L0_tok_lin_w).T, "lin_b": np.asarray(L0_tok_lin_b).reshape(D, 1),
        "wq": by_head(L0_attn_Wq), "wk": by_head(L0_attn_Wk), "wv": by_head(L0_attn_Wv),
        "bq": np.asarray(L0_attn_bq).reshape(D, 1), "bk": np.asarray(L0_attn_bk).reshape(D, 1),
        "bvo": np.stack([np.concatenate([bv, bo])] * 3), "wo": L0_attn_Wo,
        "ffn_wq": L0_ffn_Wq, "ffn_bq": np.stack([np.asarray(L0_ffn_bq)] * 3, axis=1),
        "ffn_keys_t": np.transpose(np.asarray(L0_ffn_keys), (1, 3, 0, 2)),
        "table": np.concatenate([np.asarray(L0_ffn_w_down_embed), np.asarray(L0_ffn_w_up_embed)], axis=1),
        "ident": np.eye(P, dtype=np.float32), "sel_w": sel_w.reshape(P, -1), "sel_v": sel_v,
        "part_masks": np.array([[0, 0], [1, 0], [1, 1]], np.float32),
        "iota8": np.stack([np.arange(8, dtype=np.float32)] * P),
    }
    nc = bacc.Bacc("TRN2", target_bir_lowering=False, num_devices=1)
    in_map, args = {}, []
    for name, a in arrays.items():
        a = np.ascontiguousarray(a)
        in_map[f"in_{name}"] = a
        args.append(nc.dram_tensor(f"in_{name}", a.shape, mybir.dt.from_np(a.dtype), kind="ExternalInput").ap())
    args.append(nc.dram_tensor("out_rows", (B * NPAD, D), F32, kind="ExternalOutput").ap())
    early_fusion(nc, *args)
    r = run_bass_kernel_spmd(nc, [in_map], core_ids=[0])
    return r.results[0]["out_rows"].reshape(B, NPAD, D)[:, :NTOK, :]
```
